# Optimizing a Trainium2 kernel written in Bass

```python
import numpy as np
import jax
import jax.numpy as jnp

def _softmax(x, axis=-1):
    return jax.nn.softmax(x, axis=axis)

def _gelu(x):
    return jax.nn.gelu(x, approximate=True)

def _silu(x):
    return jax.nn.silu(x)

def _sigmoid(x):
    return jax.nn.sigmoid(x)

def _layernorm(x, axis=-1, eps=1e-05):
    m = jnp.mean(x, axis=axis, keepdims=True)
    v = jnp.var(x, axis=axis, keepdims=True)
    return (x - m) / jnp.sqrt(v + eps)

def _scatter_add(tgt, idx, src, axis=0):
    return tgt.at[idx].add(src)

def _segment_sum(src, seg, n):
    return jax.ops.segment_sum(src, seg, n)
kernel_name = 'mk_gnn_preln_d1_gnn_r8_4bba0d'

def setup_inputs(seed: int=0):
    np.random.seed(seed)
    _w = jnp.asarray

    def _rec_inputs():
        import jax
        import jax.numpy as jnp
        _gk = jax.random.key(seed)
        x = -0.000202 + 1 * jax.random.normal(jax.random.fold_in(_gk, 1), (12500, 128), jnp.float32)
        src = jax.random.randint(jax.random.fold_in(_gk, 2), (400000,), 0, 12500, jnp.int32)
        dst = jnp.minimum((12500 * jax.random.uniform(jax.random.fold_in(_gk, 3), (400000,)) ** 2.0).astype(jnp.int32), 99999)
        _o = jnp.argsort(dst, stable=True)
        src = src[_o]
        dst = dst[_o]
        edge_attr_20 = jax.random.uniform(jax.random.fold_in(_gk, 12), (400000, 20), jnp.float32, 0.0, 1)
        edge_weight = jax.random.uniform(jax.random.fold_in(_gk, 13), (400000,), jnp.float32, 0.0, 0.999998)
        return (x, src, dst, edge_attr_20, edge_weight)
    x, src, dst, edge_attr_20, edge_weight = _rec_inputs()

    def _L0_gnn_setup():
        import jax, jax.numpy as jnp
        import numpy as np
        from jax.scipy.special import erf
        N_NODES = 6250
        N_EDGES = 100000
        N_BASIS = 128
        N_RBF = 20
        N_FILT = 128

        def smu(x, alpha=0.01, mu=2.5):
            return ((1 + alpha) * x + (1 - alpha) * x * erf(mu * (1 - alpha) * x)) / 2
        key = jax.random.key(seed)
        ks = jax.random.split(key, 16)
        x = jax.random.normal(ks[0], (N_NODES, N_BASIS), dtype=jnp.float32)
        f_ij = jax.random.uniform(ks[1], (N_EDGES, N_RBF), dtype=jnp.float32)
        rcut_ij = jax.random.uniform(ks[2], (N_EDGES,), dtype=jnp.float32)
        idx_i = jnp.sort(jax.random.randint(ks[3], (N_EDGES,), 0, N_NODES))
        idx_j = jax.random.randint(ks[4], (N_EDGES,), 0, N_NODES)
        s = lambda n: 1.0 / np.sqrt(n)
        W_in2f = jax.random.normal(ks[5], (N_FILT, N_BASIS), dtype=jnp.float32) * s(N_BASIS)
        W_f1 = jax.random.normal(ks[6], (N_FILT, N_RBF), dtype=jnp.float32) * s(N_RBF)
        b_f1 = jnp.zeros((N_FILT,), jnp.float32)
        W_f2 = jax.random.normal(ks[7], (N_FILT, N_FILT), dtype=jnp.float32) * s(N_FILT)
        b_f2 = jnp.zeros((N_FILT,), jnp.float32)
        W_o1 = jax.random.normal(ks[8], (N_BASIS, N_FILT), dtype=jnp.float32) * s(N_FILT)
        b_o1 = jnp.zeros((N_BASIS,), jnp.float32)
        W_o2 = jax.random.normal(ks[9], (N_BASIS, N_BASIS), dtype=jnp.float32) * s(N_BASIS)
        b_o2 = jnp.zeros((N_BASIS,), jnp.float32)
        return dict(x=x, f_ij=f_ij, rcut_ij=rcut_ij, idx_i=idx_i, idx_j=idx_j, W_in2f=W_in2f, W_f1=W_f1, b_f1=b_f1, W_f2=W_f2, b_f2=b_f2, W_o1=W_o1, b_o1=b_o1, W_o2=W_o2, b_o2=b_o2)
    _L0_gnn_all = _L0_gnn_setup()
    _L0_gnn_in = {k: v for k, v in _L0_gnn_all.items() if k in ('W_in2f', 'W_f1', 'b_f1', 'W_f2', 'b_f2', 'W_o1', 'b_o1', 'W_o2', 'b_o2')}
    del _L0_gnn_all
    return {'x': x, 'src': src, 'dst': dst, 'edge_attr_20': edge_attr_20, 'edge_weight': edge_weight, 'L0_gnn_W_in2f': _L0_gnn_in['W_in2f'], 'L0_gnn_W_f1': _L0_gnn_in['W_f1'], 'L0_gnn_b_f1': _L0_gnn_in['b_f1'], 'L0_gnn_W_f2': _L0_gnn_in['W_f2'], 'L0_gnn_b_f2': _L0_gnn_in['b_f2'], 'L0_gnn_W_o1': _L0_gnn_in['W_o1'], 'L0_gnn_b_o1': _L0_gnn_in['b_o1'], 'L0_gnn_W_o2': _L0_gnn_in['W_o2'], 'L0_gnn_b_o2': _L0_gnn_in['b_o2']}

def reference(x, src, dst, edge_attr_20, edge_weight, L0_gnn_W_in2f, L0_gnn_W_f1, L0_gnn_b_f1, L0_gnn_W_f2, L0_gnn_b_f2, L0_gnn_W_o1, L0_gnn_b_o1, L0_gnn_W_o2, L0_gnn_b_o2):
    import jax
    import jax.numpy as jnp

    def _L0_gnn_ref(x, f_ij, rcut_ij, idx_i, idx_j, W_in2f, W_f1, b_f1, W_f2, b_f2, W_o1, b_o1, W_o2, b_o2):
        import jax, jax.numpy as jnp
        import numpy as np
        from jax.scipy.special import erf
        N_NODES = 6250
        N_EDGES = 100000
        N_BASIS = 128
        N_RBF = 20
        N_FILT = 128

        def smu(x, alpha=0.01, mu=2.5):
            return ((1 + alpha) * x + (1 - alpha) * x * erf(mu * (1 - alpha) * x)) / 2
        h = x @ W_in2f.T
        Wij = smu(f_ij @ W_f1.T + b_f1) @ W_f2.T + b_f2
        Wij = Wij * rcut_ij[:, None]
        x_ij = h[idx_j] * Wij
        agg = jax.ops.segment_sum(x_ij, idx_i, num_segments=h.shape[0])
        out = smu(agg @ W_o1.T + b_o1) @ W_o2.T + b_o2
        return out
    h = jnp.maximum(_layernorm(x, axis=-1), 0.0)
    x = x + _L0_gnn_ref(h, edge_attr_20, edge_weight, src, dst, L0_gnn_W_in2f, L0_gnn_W_f1, L0_gnn_b_f1, L0_gnn_W_f2, L0_gnn_b_f2, L0_gnn_W_o1, L0_gnn_b_o1, L0_gnn_W_o2, L0_gnn_b_o2)
    return x

_drawn_inputs = setup_inputs


def setup_inputs(seed=0):
    import zlib

    import numpy as np

    out = dict(_drawn_inputs(seed))
    spreads = {'L0_gnn_b_f1': (0.0, 0.1),
     'L0_gnn_b_f2': (0.0, 0.1),
     'L0_gnn_b_o1': (0.0, 0.1),
     'L0_gnn_b_o2': (0.0, 0.1)}
    factors = {}
    for name, (base, spread) in spreads.items():
        noise = np.random.default_rng([zlib.crc32(name.encode()), seed]).standard_normal(out[name].shape)
        drawn = base * np.exp(spread * noise) if base else spread * noise
        out[name] = jnp.asarray(drawn.astype(out[name].dtype))
    for name, factor in factors.items():
        out[name] = (out[name] * factor).astype(out[name].dtype)
    return out
```

```python
import numpy as np
import concourse.bass as bass
from concourse import mybir
from contextlib import ExitStack

F32, BF16, I32 = mybir.dt.float32, mybir.dt.bfloat16, mybir.dt.int32
ALU = mybir.AluOpType
ACT = mybir.ActivationFunctionType

LANES = 128
TILES_U = 4
UNIT = LANES * TILES_U
UNITS_P = 2
PAIR = UNIT * UNITS_P
TILES_P = TILES_U * UNITS_P
BODY = 4
TABLES = TILES_P
NODE_P = 125
NODE_G = 4
SMU_S = 2.5 * 0.99 * 2 ** 0.5
SMU_W = 0.99 / SMU_S
SMU_L = 0.01 / SMU_W
EPS = 1e-5


class Count:

    def __init__(self, base, per_iter=0, i=None):
        self.base, self.per_iter, self.i = base, per_iter, i

    def value(self, times=1, plus=0):
        fixed = self.base * times + plus
        return fixed if self.i is None else self.i * (self.per_iter * times) + fixed


def wait_for(eng, sem, at, times=1, plus=0):
    v = at.value(times, plus)
    if at.i is None and v <= 0:
        return
    eng.wait_ge(sem, v)


def build(nc, n_nodes, n_edges, F, R, t):
    n_units = n_edges // UNIT
    n_pairs = n_units // UNITS_P
    n_tiles = n_edges // LANES
    n_iter = n_units // BODY
    node_tiles = n_nodes // NODE_P
    node_groups = node_tiles // NODE_G
    rows = n_nodes + LANES

    h_table = nc.dram_tensor("h_table", [n_nodes, F], F32, kind="Internal")
    tables = [nc.dram_tensor(f"sum_table{k}", [rows, F], F32, kind="Internal") for k in range(TABLES)]

    ctx = ExitStack()
    with ctx:
        def sb(name, shape, dt=F32):
            return ctx.enter_context(nc.sbuf_tensor(name, shape, dt))

        def ps(name, shape, dt=F32):
            return ctx.enter_context(nc.psum_tensor(name, shape, dt))

        def sem(name):
            return ctx.enter_context(nc.semaphore(name))

        ident = sb("ident", [LANES, LANES])
        ones_bf = sb("ones_bf", [LANES, LANES], BF16)
        zero_rows = sb("zero_rows", [LANES, 2 * F])
        tie_weight = sb("tie_weight", [LANES, 1])
        tie_limit = sb("tie_limit", [LANES, 1])
        lane = sb("lane", [LANES, 1])
        eps = sb("eps", [LANES, 1])
        w_in = sb("w_in", [F, F])
        w_f1 = sb("w_f1", [LANES, F])
        w_f2 = sb("w_f2", [F, F])
        w_o1 = sb("w_o1", [F, F])
        w_o2 = sb("w_o2", [F, F])
        b_o1 = sb("b_o1", [F, 1])
        b_o1s = sb("b_o1s", [F, 1])
        b_o2 = sb("b_o2", [LANES, F])
        b_f2 = sb("b_f2", [1, 3, F])
        b_f2_part = sb("b_f2_part", [1, 3, F], BF16)
        b_f2_rows = sb("b_f2_rows", [LANES, TILES_U, F], BF16)
        x_all = sb("x_all", [NODE_P, node_tiles, F])
        mean_var = sb("mean_var", [NODE_P, node_tiles, 2])
        stats = sb("stats", [NODE_P, node_tiles, 6])
        rstd = sb("rstd", [NODE_P, node_tiles])
        shift = sb("shift", [NODE_P, node_tiles])
        hn = sb("hn", [NODE_P, 2, NODE_G, F])
        hT = sb("hT", [F, 2, NODE_G, NODE_P])
        h_out = sb("h_out", [NODE_P, 2, NODE_G, F])
        src_i = sb("src_i", [LANES, n_tiles], I32)
        dst_i = sb("dst_i", [LANES, n_tiles + TILES_P], I32)
        META = 3
        meta = sb("meta", [LANES, META, n_tiles])
        meta_p = sb("meta_p", [LANES, 2, META, TILES_P])
        dst_p = sb("dst_p", [LANES, 2, TILES_P], I32)
        attr = sb("attr", [LANES, 2, PAIR])
        src_bc = sb("src_bc", [LANES, 2, PAIR], I32)
        hg = sb("hg", [LANES, 2, TILES_P, F])
        y_sb = sb("y_sb", [LANES, 2, TILES_P, F])
        row_idx = sb("row_idx", [LANES, 2, TILES_P], I32)
        gelu = sb("gelu", [F, 2, UNIT])
        act1 = sb("act1", [F, 2, UNIT])
        same = sb("same", [LANES, 2, TILES_U, LANES])
        msg = sb("msg", [LANES, 2, TILES_U, F])
        redirect = sb("redirect", [LANES, 2, TILES_U])

        p_z = [ps(f"p_z{v}", [LANES, UNIT]) for v in range(2)]
        p_w = [ps(f"p_w{v}", [LANES, TILES_U, F]) for v in range(2)]
        p_y = [ps(f"p_y{v}", [LANES, TILES_U, F]) for v in range(2)]
        p_tie = [ps(f"p_tie{v}", [LANES, UNIT]) for v in range(2)]

        s_ld = sem("s_ld")
        s_meta = sem("s_meta")
        s_zero = sem("s_zero")
        s_pool = sem("s_pool")
        s_dve = sem("s_dve")
        s_bf2 = sem("s_bf2")
        s_act = sem("s_act")
        s_hn, s_hT, s_hTs, s_hm, s_ho = (sem(n) for n in ("s_hn", "s_hT", "s_hTs", "s_hm", "s_ho"))
        s_hst = [sem(f"s_hst{b}") for b in range(2)]
        s_a_done = sem("s_a_done")
        s_attr = [sem(f"s_attr{q}") for q in range(2)]
        s_srcbc = [sem(f"s_srcbc{q}") for q in range(2)]
        s_hg = [sem(f"s_hg{q}") for q in range(2)]
        s_scat = [sem(f"s_scat{k}") for k in range(TABLES)]
        s_z, s_gelu, s_smu, s_w, s_msg, s_same, s_y, s_ysb, s_idx, s_rot = (
            sem(n) for n in ("s_z", "s_gelu", "s_smu", "s_w", "s_msg", "s_same", "s_y", "s_ysb", "s_idx", "s_rot"))
        s_go = sem("s_go")
        s_dst = sem("s_dst")
        s_metap = sem("s_metap")
        s_red = sem("s_red")
        s_tab = [sem(f"s_tab{b}") for b in range(2)]
        s_ot = [sem(f"s_ot{b}") for b in range(2)]
        s_sum, s_aT, s_aTs, s_u, s_oe, s_os, s_om, s_of, s_ub, s_acc = (
            sem(n) for n in ("s_sum", "s_aT", "s_aTs", "s_u", "s_oe", "s_os", "s_om", "s_of", "s_ub", "s_acc"))

        N_LD = 10
        x_view = t["x"].rearrange("(p n) f -> p n f", p=NODE_P)
        h_view = h_table[:, :].rearrange("(p n) f -> p n f", p=NODE_P)
        out_view = t["out"].rearrange("(p n) f -> p n f", p=NODE_P)
        tab_view = [tb[0:n_nodes, :].rearrange("(p n) f -> p n f", p=NODE_P) for tb in tables]
        tab_in = [hg, y_sb]

        block = ctx.enter_context(nc.Block())

        @block.sync
        def _(sp):
            sp.dma_start(x_all[:, :, :], x_view).then_inc(s_ld, 16)
            for dst, src in ((w_in[:, :], t["w_inT"]), (w_f2[:, :], t["w_f2T"]),
                             (w_o1[:, :], t["w_o1T"]), (w_o2[:, :], t["w_o2T"]),
                             (b_o1[:, :], t["b_o1"]), (b_f2[0:1, 0, :], t["b_f2"]),
                             (b_o2[:, :], t["b_o2"].partition_broadcast(LANES))):
                sp.dma_start(dst, src).then_inc(s_ld, 16)
            sp.wait_ge(s_pool, 1)
            sp.dma_start(w_f1[0:R, :], t["w_f1T"]).then_inc(s_ld, 16)
            sp.dma_start(w_f1[R:R + 1, :], t["b_f1"]).then_inc(s_ld, 16)
            sp.dma_start(src_i[:, :], t["src_col"]).then_inc(s_meta, 16)
            sp.dma_start(dst_i[:, 0:n_tiles], t["dst_col"]).then_inc(s_meta, 16)
            sp.dma_start(meta[:, 2, :], t["weight_col"]).then_inc(s_meta, 16)
            sp.wait_ge(s_dve, 3)
            for part in range(3):
                for k in range(TILES_U):
                    sp.dma_start(b_f2_rows[part:part + 1, k, :], b_f2_part[0:1, part, :]).then_inc(s_bf2, 16)
            with sp.Fori(0, node_groups) as g:
                sp.wait_ge(s_ho, g + 1)
                sp.dma_start(h_view[:, bass.ds(g * NODE_G, NODE_G), :],
                             h_out[:, 0, :, :]).then_inc(s_hst[0], 16)
                sp.wait_ge(s_hst[0], (g + 1) * 16)
                sp.sem_inc(s_a_done, 1)

            def load_pair(p, q):
                wait_for(sp, s_z, p, 2, -2)
                sp.dma_start(attr[0:R, q, :], t["attrT"][:, bass.ds(p.value() * PAIR, PAIR)]).then_inc(s_attr[q], 16)
                wait_for(sp, s_same, p, 2, -2)
                sp.dma_start(src_bc[:, q, :],
                             t["src"][:, bass.ds(p.value() * PAIR, PAIR)].partition_broadcast(LANES)).then_inc(s_srcbc[q], 16)

            sp.wait_ge(s_pool, 2)
            for q in range(2):
                load_pair(Count(q), q)
            with sp.Fori(1, n_iter) as i:
                for q in range(2):
                    load_pair(Count(q, 2, i), q)

            with sp.Fori(0, node_groups) as g:
                sp.wait_ge(s_of, g + 1)
                sp.dma_start(out_view[:, bass.ds(g * NODE_G, NODE_G), :], h_out[:, 0, :, :]).then_inc(s_ot[0], 16)
                sp.wait_ge(s_ot[0], (g + 1) * 16)
                sp.sem_inc(s_acc, 1)

        @block.gpsimd
        def _(pool):
            pool.memset(w_f1[:, :], 0.0).then_inc(s_pool, 1)
            pool.memset(attr[:, :, :], 1.0).then_inc(s_pool, 1)
            pool.memset(zero_rows[:, :], 0.0)
            pool.memset(ones_bf[:, :], 1.0)
            pool.memset(eps[:, :], EPS)
            pool.memset(b_f2_rows[:, :, :], 0.0)
            pool.iota(lane[:, :], pattern=[[0, 1]], base=0, channel_multiplier=1,
                      allow_small_or_imprecise_dtypes=True)
            pool.memset(dst_i[:, n_tiles:], 0)
            pool.memset(ident[:, :], 0.0).then_inc(s_pool, 1)
            pool.wait_ge(s_pool, 3)
            pool.affine_select(out=ident[:, :], in_=ident[:, :], compare_op=ALU.not_equal, fill=1.0, base=0,
                               pattern=[[-1, LANES]], channel_multiplier=1).then_inc(s_pool, 1)
            pool.wait_ge(s_pool, 4)
            for k, tb in enumerate(tables):
                whole = rows // (2 * LANES)
                flat = tb[0:whole * 2 * LANES, :].rearrange("(n p two) f -> p n (two f)", p=LANES, two=2)
                pool.dma_start(flat, zero_rows[:, :].unsqueeze(1).to_broadcast([LANES, whole, 2 * F])).then_inc(s_zero, 16)
                left = rows - whole * 2 * LANES
                if left:
                    pool.dma_start(tb[whole * 2 * LANES:rows, :], zero_rows[0:left, 0:F]).then_inc(s_zero, 16)
            pool.wait_ge(s_zero, 16 * TABLES * (2 if rows % (2 * LANES) else 1))
            pool.wait_ge(s_a_done, node_groups)

            def gather(p, q):
                wait_for(pool, s_dst, p, 1, 1)
                pool.sem_inc(s_go, 1)
                for k in range(TILES_P):
                    pool.indirect_dma_start(out=hg[:, q, k, :], out_offset=None, in_=h_table[:, :],
                                            in_offset=bass.IndirectOffsetOnAxis(ap=dst_p[:, q, k:k + 1], axis=0),
                                            ).then_inc(s_hg[q], 16)

            def scatter(p, q):
                for v in range(UNITS_P):
                    wait_for(pool, s_idx, p, 2, v + 1)
                    wait_for(pool, s_ysb, p, 2, v + 1)
                    for k in range(v * TILES_U, (v + 1) * TILES_U):
                        wait_for(pool, s_scat[k], p, 16)
                    pool.sem_inc(s_rot, 1)
                    for k in range(v * TILES_U, (v + 1) * TILES_U):
                        pool.indirect_dma_start(out=tables[k][:, :],
                                                out_offset=bass.IndirectOffsetOnAxis(ap=row_idx[:, q, k:k + 1], axis=0),
                                                in_=y_sb[:, q, k, :], in_offset=None,
                                                compute_op=ALU.add).then_inc(s_scat[k], 16)

            gather(Count(0), 0)
            gather(Count(1), 1)
            scatter(Count(0), 0)
            with pool.Fori(1, n_iter) as i:
                gather(Count(0, 2, i), 0)
                scatter(Count(-1, 2, i), 1)
                gather(Count(1, 2, i), 1)
                scatter(Count(0, 2, i), 0)
            scatter(Count(n_pairs - 1), 1)
            for k in range(TABLES):
                pool.wait_ge(s_scat[k], 16 * n_pairs)
            with pool.Fori(0, node_groups) as g:
                pool.wait_ge(s_sum, g)
                for k in range(TABLES):
                    pool.dma_start(tab_in[k // 4][0:NODE_P, (k // 2) % 2, (k % 2) * 4:(k % 2) * 4 + 4, :],
                                   tab_view[k][:, bass.ds(g * NODE_G, NODE_G), :]).then_inc(s_tab[0], 16)

        @block.scalar
        def _(act):
            act.wait_ge(s_dve, 4)
            act.wait_ge(s_pool, 4)
            act.activation(rstd[:, :], mean_var[:, :, 1], ACT.Sqrt, bias=eps[0:NODE_P, :]).then_inc(s_act, 1)
            act.wait_ge(s_dve, 6)
            with act.Fori(0, node_groups) as g:
                act.wait_ge(s_hT, g)
                for k in range(NODE_G):
                    last = act.activation(hn[:, 0, k, :], x_all[:, bass.ds(g * NODE_G + k, 1), :].rearrange("p a f -> p (a f)"),
                                          ACT.Relu, bias=shift[:, bass.ds(g * NODE_G + k, 1)],
                                          scale=rstd[:, bass.ds(g * NODE_G + k, 1)])
                last.then_inc(s_hn, 1)
                act.wait_ge(s_hm, g + 1)
                act.wait_ge(s_a_done, g)
                act.copy(h_out[:, 0, :, :], p_w[0][0:NODE_P, :, :]).then_inc(s_ho, 1)

            def gelu_of(n, v):
                wait_for(act, s_z, n, 1, 1)
                wait_for(act, s_smu, n, 1, -1)
                act.activation(gelu[:, v, :], p_z[v][:, :], ACT.Gelu, scale=SMU_S).then_inc(s_gelu, 1)

            def rows_out(n, q, v):
                wait_for(act, s_y, n, 1, 1)
                wait_for(act, s_rot, n, 1, -1)
                act.copy(y_sb[:, q, v * TILES_U:(v + 1) * TILES_U, :], p_y[v][:, :, :]).then_inc(s_ysb, 1)

            def step(n, c, do_gelu=True):
                if do_gelu:
                    gelu_of(n, c % 2)
                if n.i is not None or n.base >= 2:
                    rows_out(Count(n.base - 2, n.per_iter, n.i), ((c - 2) // 2) % 2, c % 2)

            for c in range(BODY):
                step(Count(c), c)
            with act.Fori(1, n_iter) as i:
                for c in range(BODY):
                    step(Count(c, BODY, i), c)
            for c in range(2):
                step(Count(n_units + c), c, do_gelu=False)
            with act.Fori(0, node_groups) as g:
                act.wait_ge(s_u, g + 1)
                act.activation(gelu[:, 0, 0:NODE_G * NODE_P], p_z[1][:, 0:NODE_G * NODE_P], ACT.Gelu,
                               scale=SMU_S, bias=b_o1s[:, :]).then_inc(s_oe, 1)

        @block.vector
        def _(dve):
            dve.wait_ge(s_ld, 16 * N_LD)
            dve.wait_ge(s_pool, 4)
            dve.tensor_copy(b_f2_part[0:1, 0, :], b_f2[0:1, 0, :]).then_inc(s_dve, 1)
            dve.wait_ge(s_dve, 1)
            dve.tensor_tensor(b_f2[0:1, 1, :], b_f2[0:1, 0, :], b_f2_part[0:1, 0, :], ALU.subtract).then_inc(s_red, 1)
            dve.wait_ge(s_red, 1)
            dve.tensor_copy(b_f2_part[0:1, 1, :], b_f2[0:1, 1, :]).then_inc(s_dve, 1)
            dve.wait_ge(s_dve, 2)
            dve.tensor_tensor(b_f2[0:1, 2, :], b_f2[0:1, 1, :], b_f2_part[0:1, 1, :], ALU.subtract).then_inc(s_red, 1)
            dve.wait_ge(s_red, 2)
            dve.tensor_copy(b_f2_part[0:1, 2, :], b_f2[0:1, 2, :]).then_inc(s_dve, 1)
            for n in range(node_tiles):
                last = dve.bn_stats(stats[:, n, :], x_all[:, n, :])
            last.then_inc(s_red, 1)
            dve.wait_ge(s_red, 3)
            for n in range(node_tiles):
                last = dve.bn_aggr(mean_var[:, n, :], stats[:, n, :])
            last.then_inc(s_dve, 1)
            dve.wait_ge(s_act, 1)
            dve.reciprocal(rstd[:, :], rstd[:, :]).then_inc(s_dve, 1)
            dve.wait_ge(s_dve, 5)
            dve.scalar_tensor_tensor(shift[:, :], mean_var[:, :, 0], -1.0, rstd[:, :], ALU.mult, ALU.mult).then_inc(s_dve, 1)
            dve.tensor_scalar(w_f2[:, :], w_f2[:, :], SMU_W, None, ALU.mult)
            dve.tensor_scalar(w_o2[:, :], w_o2[:, :], SMU_W, None, ALU.mult)
            dve.tensor_scalar(b_o1s[:, :], b_o1[:, :], SMU_S, None, ALU.mult)
            dve.tensor_scalar(tie_limit[:, :].bitcast(I32), lane[:, :], -1.0, 190.0, ALU.mult, ALU.add).then_inc(s_red, 1)
            dve.wait_ge(s_red, 4)
            dve.tensor_scalar(tie_weight[:, :].bitcast(I32), tie_limit[:, :].bitcast(I32), 23, None,
                              ALU.logical_shift_left).then_inc(s_red, 1)
            dve.wait_ge(s_red, 5)
            dve.tensor_scalar(tie_limit[:, :], tie_weight[:, :], 2.5, None, ALU.mult)
            dve.tensor_scalar(lane[:, :], lane[:, :], float(n_nodes), None, ALU.add).then_inc(s_red, 1)
            dve.wait_ge(s_red, 6)
            dve.wait_ge(s_meta, 48)
            dve.tensor_copy(meta[:, 0, :], src_i[:, :])
            dve.tensor_scalar(meta[:, 1, :], src_i[:, :], -1.0, lane[:, :], ALU.mult, ALU.add).then_inc(s_dve, 1)
            dve.wait_ge(s_dve, 7)
            with dve.Fori(0, node_groups) as g:
                dve.wait_ge(s_hT, g + 1)
                dve.wait_ge(s_hm, g)
                dve.tensor_copy(hT[:, 0, :, :], p_y[0][:, :, 0:NODE_P]).then_inc(s_hTs, 1)
            dve.wait_ge(s_ho, node_groups)
            dve.tensor_tensor(x_all[:, :, :], x_all[:, :, :],
                              b_o2[0:NODE_P, :].unsqueeze(1).to_broadcast([NODE_P, node_tiles, F]), ALU.add)

            def pair_meta(p, q):
                wait_for(dve, s_idx, p, 2, -2)
                dve.tensor_copy(meta_p[:, q, :, :], meta[:, :, bass.ds(p.value() * TILES_P, TILES_P)]).then_inc(s_metap, 1)
                wait_for(dve, s_metap, p, 1, 1)

            def pair_dst(p, q):
                dve.tensor_copy(dst_p[:, q, :], dst_i[:, bass.ds(p.value() * TILES_P, TILES_P)]).then_inc(s_dst, 1)

            def same_source(n, p, q, v):
                cols = slice(v * TILES_U, (v + 1) * TILES_U)
                if v == 0:
                    wait_for(dve, s_srcbc[q], Count(p.base // 2, p.per_iter // 2, p.i), 16, 16)
                wait_for(dve, s_y, n, 1, -1)
                dve.tensor_tensor(same[:, v, :, :],
                                  src_bc[:, q, v * UNIT:(v + 1) * UNIT].rearrange("p (k e) -> p k e", k=TILES_U),
                                  meta_p[:, q, 0, cols].unsqueeze(2).to_broadcast([LANES, TILES_U, LANES]),
                                  ALU.is_equal).then_inc(s_same, 1)

            def smu(n, v):
                wait_for(dve, s_gelu, n, 1, 1)
                wait_for(dve, s_w, n, 1, -1)
                dve.scalar_tensor_tensor(act1[:, v, :], p_z[v][:, :], SMU_L, gelu[:, v, :], ALU.mult, ALU.add).then_inc(s_smu, 1)

            def message(n, p, q, v):
                wait_for(dve, s_w, n, 1, 1)
                if v == 0:
                    wait_for(dve, s_hg[q], Count(p.base // 2, p.per_iter // 2, p.i), 16 * TILES_P, 16 * TILES_P)
                wait_for(dve, s_y, n, 1, -1)
                for k in range(TILES_U):
                    kk = v * TILES_U + k
                    last = dve.scalar_tensor_tensor(msg[:, v, k, :], p_w[v][:, k, :], meta_p[:, q, 2, kk:kk + 1],
                                                    hg[:, q, kk, :], ALU.mult, ALU.mult)
                last.then_inc(s_msg, 1)

            def row_numbers(n, q, v):
                cols = slice(v * TILES_U, (v + 1) * TILES_U)
                wait_for(dve, s_y, n, 1, 1)
                wait_for(dve, s_rot, n, 1, -1)
                dve.scalar_tensor_tensor(redirect[:, v, :], p_tie[v][:, 0:TILES_U], tie_limit[:, :], meta_p[:, q, 1, cols],
                                         ALU.is_gt, ALU.mult).then_inc(s_red, 1)
                wait_for(dve, s_red, n, 1, 7)
                dve.tensor_tensor(row_idx[:, q, cols], redirect[:, v, :], meta_p[:, q, 0, cols], ALU.add).then_inc(s_idx, 1)

            def step(i, c, base, new=True):
                def unit(back):
                    return Count(base + c - back, BODY if i is not None else 0, i)

                def pair(back):
                    return Count((base + c - back) // 2, 2 if i is not None else 0, i)

                q0, q1, q2 = ((c - b) // 2 % 2 for b in range(3))
                v0, v1, v2 = ((c - b) % 2 for b in range(3))
                if new and c % 2 == 0:
                    pair_meta(pair(0), q0)
                if new:
                    same_source(unit(0), pair(0), q0, v0)
                    smu(unit(0), v0)
                if i is not None or 1 <= base + c <= n_units:
                    message(unit(1), pair(1), q1, v1)
                if new and c % 2 == 0 and not (i is None and base + c + 2 >= n_units):
                    pair_dst(pair(-2), (q0 + 1) % 2)
                if i is not None or base + c >= 2:
                    row_numbers(unit(2), q2, v2)

            dve.tensor_copy(dst_p[:, 0, :], dst_i[:, 0:TILES_P]).then_inc(s_dst, 1)
            for c in range(BODY):
                step(None, c, 0)
            with dve.Fori(1, n_iter) as i:
                for c in range(BODY):
                    step(i, c, 0)
            for c in range(2):
                step(None, c, n_units, new=False)

            acc = msg[0:NODE_P, 0, :, :]
            act1n = act1[:, 0, 0:NODE_G * NODE_P]
            zb = act1[:, 1, 0:NODE_G * NODE_P]
            with dve.Fori(0, node_groups) as g:
                dve.wait_ge(s_tab[0], (g + 1) * (16 * TABLES))
                dve.wait_ge(s_aT, g)
                for k in range(1, TABLES):
                    prev = tab_in[0][0:NODE_P, 0, 0:4, :] if k == 1 else acc
                    ins = dve.tensor_tensor(acc, prev, tab_in[k // 4][0:NODE_P, (k // 2) % 2, (k % 2) * 4:(k % 2) * 4 + 4, :], ALU.add)
                    ins.then_inc(s_ub, 1)
                    dve.wait_ge(s_ub, g * (TABLES - 1) + k)
                dve.sem_inc(s_sum, 1)
                dve.wait_ge(s_aT, g + 1)
                dve.wait_ge(s_u, g)
                dve.tensor_copy(hT[:, 0, :, :], p_y[0][:, :, 0:NODE_P]).then_inc(s_aTs, 1)
                dve.wait_ge(s_oe, g + 1)
                dve.tensor_scalar(zb, p_z[1][:, 0:NODE_G * NODE_P], b_o1[:, :], None, ALU.add).then_inc(s_red, 1)
                dve.wait_ge(s_red, g + (6 + n_units + 1))
                dve.wait_ge(s_om, g)
                dve.scalar_tensor_tensor(act1n, zb, SMU_L, gelu[:, 0, 0:NODE_G * NODE_P], ALU.mult, ALU.add).then_inc(s_os, 1)
                dve.wait_ge(s_om, g + 1)
                dve.wait_ge(s_acc, g)
                dve.tensor_tensor(h_out[:, 0, :, :], p_w[0][0:NODE_P, :, :], x_all[:, bass.ds(g * NODE_G, NODE_G), :],
                                  ALU.add).then_inc(s_of, 1)

        @block.tensor
        def _(pe):
            pe.wait_ge(s_ld, 16 * N_LD)
            pe.wait_ge(s_pool, 4)
            with pe.Fori(0, node_groups) as g:
                pe.wait_ge(s_hn, g + 1)
                pe.wait_ge(s_hTs, g)
                for k in range(NODE_G):
                    last = pe.transpose(p_y[0][:, k, 0:NODE_P], hn[:, 0, k, :], ident[0:NODE_P, 0:NODE_P])
                last.then_inc(s_hT, 1)
                pe.wait_ge(s_hTs, g + 1)
                pe.wait_ge(s_ho, g)
                for k in range(NODE_G):
                    last = pe.matmul(p_w[0][0:NODE_P, k, :], hT[:, 0, k, :], w_in[:, :], start=True, stop=True)
                last.then_inc(s_hm, 1)
            pe.wait_ge(s_hTs, node_groups)
            pe.wait_ge(s_ho, node_groups)
            pe.wait_ge(s_dve, 7)
            pe.wait_ge(s_bf2, 16 * 3 * TILES_U)

            def filter1(n, p, q, v):
                if v == 0:
                    wait_for(pe, s_attr[q], Count(p.base // 2, p.per_iter // 2, p.i), 16, 16)
                wait_for(pe, s_smu, n, 1, -1)
                pe.matmul(p_z[v][:, :], w_f1[:, :], attr[:, q, v * UNIT:(v + 1) * UNIT], start=True, stop=True).then_inc(s_z, 1)

            def filter2(n, v):
                wait_for(pe, s_smu, n, 1, 1)
                wait_for(pe, s_msg, n, 1, -1)
                pe.matmul(p_w[v][:, :, :], ones_bf[:, :], b_f2_rows[:, :, :], start=True, stop=False)
                for k in range(TILES_U):
                    last = pe.matmul(p_w[v][:, k, :], act1[:, v, k * LANES:(k + 1) * LANES], w_f2[:, :],
                                     start=False, stop=(k == TILES_U - 1))
                last.then_inc(s_w, 1)

            def sum_same(n, v):
                wait_for(pe, s_msg, n, 1, 1)
                wait_for(pe, s_same, n, 1, 1)
                wait_for(pe, s_idx, n, 1, -1)
                wait_for(pe, s_ysb, n, 1, -1)
                for k in range(TILES_U):
                    pe.matmul(p_tie[v][:, k:k + 1], same[:, v, k, :], tie_weight[:, :], start=True, stop=True)
                    last = pe.matmul(p_y[v][:, k, :], same[:, v, k, :], msg[:, v, k, :], start=True, stop=True)
                last.then_inc(s_y, 1)

            def step(i, c, base, new=True):
                def unit(back):
                    return Count(base + c - back, BODY if i is not None else 0, i)

                if new:
                    filter1(unit(0), Count((base + c) // 2, 2 if i is not None else 0, i), c // 2 % 2, c % 2)
                if i is not None or 1 <= base + c <= n_units:
                    filter2(unit(1), (c - 1) % 2)
                if i is not None or base + c >= 2:
                    sum_same(unit(2), c % 2)

            for c in range(BODY):
                step(None, c, 0)
            with pe.Fori(1, n_iter) as i:
                for c in range(BODY):
                    step(i, c, 0)
            for c in range(2):
                step(None, c, n_units, new=False)
            pe.wait_ge(s_ysb, n_units)
            with pe.Fori(0, node_groups) as g:
                pe.wait_ge(s_sum, g + 1)
                pe.wait_ge(s_aTs, g)
                for k in range(NODE_G):
                    last = pe.transpose(p_y[0][:, k, 0:NODE_P], msg[0:NODE_P, 0, k, :], ident[0:NODE_P, 0:NODE_P])
                last.then_inc(s_aT, 1)
                pe.wait_ge(s_aTs, g + 1)
                pe.wait_ge(s_os, g)
                pe.matmul(p_z[1][:, 0:NODE_G * NODE_P], w_o1[:, :], hT[:, 0, :, :], start=True, stop=True).then_inc(s_u, 1)
                pe.wait_ge(s_os, g + 1)
                pe.wait_ge(s_of, g)
                for k in range(NODE_G):
                    last = pe.matmul(p_w[0][0:NODE_P, k, :], act1[:, 0, k * NODE_P:(k + 1) * NODE_P], w_o2[:, :],
                                     start=True, stop=True)
                last.then_inc(s_om, 1)


def kernel(**inputs):
    import concourse.bacc as bacc
    from concourse.bass_utils import run_bass_kernel_spmd as run

    x = np.asarray(inputs["x"])
    n_nodes, F = x.shape
    attr = np.asarray(inputs["edge_attr_20"])
    n_edges, R = attr.shape
    padded = -(-n_edges // (BODY * UNIT)) * (BODY * UNIT)

    def pad(a):
        out = np.zeros((padded,) + a.shape[1:], a.dtype)
        out[:n_edges] = a
        return out

    def col(a):
        return np.ascontiguousarray(pad(np.asarray(a)).reshape(-1, LANES).T)

    g = {k[len("L0_gnn_"):]: np.asarray(v) for k, v in inputs.items() if k.startswith("L0_gnn_")}
    arrays = {
        "x": np.ascontiguousarray(x),
        "attrT": np.ascontiguousarray(pad(attr).T),
        "src": pad(np.asarray(inputs["src"])).reshape(1, -1),
        "src_col": col(inputs["src"]),
        "dst_col": col(inputs["dst"]),
        "weight_col": col(inputs["edge_weight"]),
        "w_inT": np.ascontiguousarray(g["W_in2f"].T),
        "w_f1T": np.ascontiguousarray(g["W_f1"].T),
        "w_f2T": np.ascontiguousarray(g["W_f2"].T),
        "w_o1T": np.ascontiguousarray(g["W_o1"].T),
        "w_o2T": np.ascontiguousarray(g["W_o2"].T),
        "b_f1": g["b_f1"].reshape(1, F),
        "b_f2": g["b_f2"].reshape(1, F),
        "b_o1": g["b_o1"].reshape(F, 1),
        "b_o2": g["b_o2"].reshape(1, F),
    }
    nc = bacc.Bacc("TRN2", target_bir_lowering=False, num_devices=1)
    t = {k: nc.dram_tensor(f"in_{k}", a.shape, mybir.dt.from_np(a.dtype), kind="ExternalInput").ap()
         for k, a in arrays.items()}
    t["out"] = nc.dram_tensor("out", (n_nodes, F), F32, kind="ExternalOutput").ap()
    build(nc, n_nodes, padded, F, R, t)
    r = run(nc, [{f"in_{k}": a for k, a in arrays.items()}], core_ids=[0])
    return r.results[0]["out"]
```

```python
import numpy as np
import concourse.bass as bass
from concourse import mybir
from contextlib import ExitStack

F32, BF16, I32, U16 = mybir.dt.float32, mybir.dt.bfloat16, mybir.dt.int32, mybir.dt.uint16
ALU = mybir.AluOpType
ACT = mybir.ActivationFunctionType
AX = mybir.AxisListType

LANES = 128
TILES_U = 4
UNIT = LANES * TILES_U
UNITS_P = 2
PAIR = UNIT * UNITS_P
TILES_P = TILES_U * UNITS_P
BODY = 4
TABLES = 8
PARTS = 3
WINDOW = LANES
BANK = 512
NODE_P = 112
NODE_G = 4
GROUP = NODE_G * NODE_P
SMU_S = 2.5 * 0.99 * 2 ** 0.5
SMU_W = 0.99 / SMU_S
SMU_L = 0.01 / SMU_W
EPS = 1e-5


class Count:

    def __init__(self, base, per_iter=0, i=None):
        self.base, self.per_iter, self.i = base, per_iter, i

    def value(self, times=1, plus=0):
        fixed = self.base * times + plus
        return fixed if self.i is None else self.i * (self.per_iter * times) + fixed

    def halved(self):
        return Count(self.base // 2, self.per_iter // 2, self.i)


def wait_for(eng, sem, at, times=1, plus=0):
    v = at.value(times, plus)
    if at.i is None and v <= 0:
        return
    eng.wait_ge(sem, v)


def build(nc, n_nodes, n_edges, F, R, t):
    n_units = n_edges // UNIT
    n_pairs = n_units // UNITS_P
    n_tiles = n_edges // LANES
    n_iter = n_units // BODY
    rows_l = -(-n_nodes // (NODE_P * 2 * NODE_G)) * 2 * NODE_G
    n_groups = rows_l // NODE_G
    n_pad = NODE_P * rows_l
    full_lanes, last_rows = divmod(n_nodes, rows_l)
    spray = full_lanes // 16 * 16
    t_rows = -(-(n_pad + LANES) // LANES)
    dump = n_pad
    DVE_TABLES = TABLES // 2 + 1
    SEG_PAIRS = 4
    seg_lanes = n_pairs // SEG_PAIRS
    SEG = SEG_PAIRS * PAIR

    h3 = nc.dram_tensor("h3", [n_pad, PARTS * F], BF16, kind="Internal")
    tables = [nc.dram_tensor(f"sum_table{k}", [t_rows * LANES, F], F32, kind="Internal") for k in range(TABLES)]
    ends16 = nc.dram_tensor("ends16", [2, n_edges], U16, kind="Internal")
    win_dram = nc.dram_tensor("win_dram", [1, 2, n_pairs], I32, kind="Internal")

    ctx = ExitStack()
    with ctx:
        def sb(name, shape, dt=F32, stack=ctx):
            return stack.enter_context(nc.sbuf_tensor(name, shape, dt))

        def ps(name, shape, dt=F32):
            return ctx.enter_context(nc.psum_tensor(name, shape, dt))

        def sem(name):
            return ctx.enter_context(nc.semaphore(name))

        ident = sb("ident", [LANES, LANES])
        ident_bf = sb("ident_bf", [LANES, LANES], BF16)
        ones_bf = sb("ones_bf", [LANES, BANK], BF16)
        tie_weight = sb("tie_weight", [LANES, 1])
        tie_limit = sb("tie_limit", [LANES, 1])
        lane = sb("lane", [LANES, 1])
        dump_row = sb("dump_row", [LANES, 1])
        eps = sb("eps", [LANES, 1])
        w_in = sb("w_in", [F, F])
        w_f1 = sb("w_f1", [LANES, F])
        w_f2 = sb("w_f2", [F, F])
        w_o1 = sb("w_o1", [F, F])
        w_o2 = sb("w_o2", [F, F])
        b_o2 = sb("b_o2", [LANES, F])
        bias = sb("bias", [1, PARTS, 2, F])
        bias_part = sb("bias_part", [1, PARTS, 2, F], BF16)
        b_f2_rows = sb("b_f2_rows", [LANES, TILES_U, F], BF16)
        b_o1_rows = sb("b_o1_rows", [LANES, F], BF16)
        x_all = sb("x_all", [NODE_P, rows_l, F])
        mean_var = sb("mean_var", [NODE_P, rows_l, 2])
        stats = sb("stats", [NODE_P, 2, NODE_G, 6])
        mean_var_g = sb("mean_var_g", [NODE_P, 2, NODE_G, 2])
        rstd = sb("rstd", [NODE_P, rows_l])
        shift = sb("shift", [NODE_P, rows_l])
        hn = sb("hn", [NODE_P, 2, NODE_G, F])
        hT = sb("hT", [F, 2, NODE_G, NODE_P])
        h_rest = sb("h_rest", [NODE_P, 2, NODE_G, F])
        h_parts = sb("h_parts", [NODE_P, 2, NODE_G, PARTS, F], BF16)
        SRC, WEIGHT = 0, 1
        meta = sb("meta", [LANES, 2, n_tiles])
        win_first = sb("win_first", [1, 2, n_pairs], I32)
        win_row = sb("win_row", [LANES, n_pairs])
        win_i = sb("win_i", [LANES, n_pairs], I32)
        reach = sb("reach", [1, 1])
        general = sb("general", [1, 1], I32)
        seg_min = sb("seg_min", [seg_lanes, 2, SEG_PAIRS])
        seg_win = sb("seg_win", [seg_lanes, 2, SEG_PAIRS], I32)
        DUMP = 2
        meta_p = sb("meta_p", [LANES, 2, 3, TILES_P])
        dst_p = sb("dst_p", [LANES, 2, TILES_P], I32)
        row_idx = sb("row_idx", [LANES, 2, TILES_P], I32)
        redirect = sb("redirect", [LANES, 2, TILES_U])
        attr = sb("attr", [LANES, 2, PAIR])
        win = sb("win", [LANES, 2, TILES_P, PARTS * F], BF16)
        FT = F + 1
        msg = sb("msg", [LANES, 2, TILES_U, FT])
        with ExitStack() as stage:
            seg_i = sb("seg_i", [seg_lanes, SEG], I32, stage)
            seg_u = sb("seg_u", [seg_lanes, 2, SEG], U16, stage)
        with ExitStack() as late:
            tab_in = sb("tab_in", [NODE_P, 2, TABLES, NODE_G, F], F32, late)
        ends = sb("ends", [LANES, 2, 2, PAIR], U16)
        y_sb = sb("y_sb", [LANES, 2, TILES_P, F])
        gelu = sb("gelu", [F, 2, UNIT])
        act1 = sb("act1", [F, 2, UNIT])
        same = sb("same", [LANES, 2, TILES_U, LANES])
        pick = sb("pick", [LANES, 2, UNIT], BF16)
        hg = sb("hg", [LANES, 2, TILES_U, F])

        p_z = ps("p_z", [LANES, BANK])
        p_w = [ps(f"p_w{v}", [LANES, TILES_U, F]) for v in range(2)]
        p_h = ps("p_h", [LANES, TILES_U, F])
        p_y = [ps(f"p_y{v}", [LANES, TILES_U, BANK // 2]) for v in range(2)]

        s_x = sem("s_x")
        s_ld = sem("s_ld")
        s_seg = sem("s_seg")
        s_meta = sem("s_meta")
        s_zero = sem("s_zero")
        s_pool = sem("s_pool")
        s_dve = sem("s_dve")
        s_red = sem("s_red")
        s_part = sem("s_part")
        s_mv = sem("s_mv")
        s_sqrt = sem("s_sqrt")
        s_carry_v = sem("s_carry_v")
        s_carry = sem("s_carry")
        s_e16 = sem("s_e16")
        s_win_st, s_win_ld = sem("s_win_st"), sem("s_win_ld")
        s_flag = sem("s_flag")
        s_hn, s_hT, s_hTs, s_hm, s_h0, s_hr, s_h1, s_h2 = (
            sem(n) for n in ("s_hn", "s_hT", "s_hTs", "s_hm", "s_h0", "s_hr", "s_h1", "s_h2"))
        s_hst = [sem(f"s_hst{b}") for b in range(2)]
        s_attr = [sem(f"s_attr{q}") for q in range(2)]
        s_ends = [sem(f"s_ends{q}") for q in range(2)]
        s_win = [sem(f"s_win{q}") for q in range(2)]
        s_dst = [sem(f"s_dst{q}") for q in range(2)]
        s_scat = [sem(f"s_scat{k}") for k in range(TABLES)]
        s_z, s_gelu, s_smu, s_w, s_pick, s_ph, s_hg, s_msg, s_same, s_y, s_idx, s_ysb, s_rot = (
            sem(n) for n in ("s_z", "s_gelu", "s_smu", "s_w", "s_pick", "s_ph", "s_hg", "s_msg", "s_same", "s_y",
                             "s_idx", "s_ysb", "s_rot"))
        s_metap = sem("s_metap")
        s_tie = sem("s_tie")
        s_go = sem("s_go")
        s_tab = [sem(f"s_tab{b}") for b in range(2)]
        s_tab2 = [sem(f"s_tab2{b}") for b in range(2)]
        s_out = sem("s_out")
        s_sum, s_add, s_aT, s_aTs, s_u, s_oe, s_os, s_om, s_of, s_xb = (
            sem(n) for n in ("s_sum", "s_add", "s_aT", "s_aTs", "s_u", "s_oe", "s_os", "s_om", "s_of", "s_xb"))

        N_LD = 8
        x_rows = t["x"][0:full_lanes * rows_l, :].rearrange("(p n) f -> p n f", n=rows_l)
        out_rows = t["out"][0:full_lanes * rows_l, :].rearrange("(p n) f -> p n f", n=rows_l)
        h3_view = h3[:, :].rearrange("(p n) f -> p n f", p=NODE_P)
        tab_view = [tb[0:n_pad, :].rearrange("(p n) f -> p n f", p=NODE_P) for tb in tables]
        lots = [(0, spray), (spray, full_lanes)]

        def groups_loop(eng, body):
            body(Count(0), 0)
            body(Count(1), 1)
            with eng.Fori(1, n_groups // 2) as i:
                body(Count(0, 2, i), 0)
                body(Count(1, 2, i), 1)

        def edge_loop(eng, step):
            for c in range(BODY):
                step(None, c, 0)
            with eng.Fori(1, n_iter) as i:
                for c in range(BODY):
                    step(i, c, 0)
            for c in range(2):
                step(None, c, n_units)

        class Step:

            def __init__(self, i, c, base):
                self.i, self.c, self.base = i, c, base

            def has(self, back):
                return self.i is not None or 0 <= self.base + self.c - back < n_units

            def unit(self, back=0):
                return Count(self.base + self.c - back, BODY if self.i is not None else 0, self.i)

            def pair(self, back=0):
                return Count((self.base + self.c - back) // 2, 2 if self.i is not None else 0, self.i)

            def q(self, back=0):
                return (self.c - back) // 2 % 2

            def v(self, back=0):
                return (self.c - back) % 2

        block = ctx.enter_context(nc.Block())

        def either(eng, program):
            eng.wait_ge(s_flag, 1)
            anywhere = eng.value_load(general[0:1, 0:1], min_val=0, max_val=1)
            with eng.If(anywhere):
                program(True)
            with eng.Else():
                program(False)

        @block.sync
        def _(sp):
            sp.wait_ge(s_xb, 1)
            for lo, hi in lots:
                sp.dma_start(x_all[lo:hi, :, :], x_rows[lo:hi, :, :]).then_inc(s_x, 16)
            sp.dma_start(x_all[full_lanes:full_lanes + 1, 0:last_rows, :],
                         t["x"][full_lanes * rows_l:n_nodes, :].rearrange("(p n) f -> p n f", p=1)).then_inc(s_x, 16)
            sp.dma_start(seg_i[:, :], t["src_seg"]).then_inc(s_seg, 16)
            for dst, src in ((w_in[:, :], t["w_inT"]), (w_f2[:, :], t["w_f2T"]),
                             (w_o1[:, :], t["w_o1T"]), (w_o2[:, :], t["w_o2T"]),
                             (bias[0:1, 0, :, :], t["bias2"]),
                             (b_o2[:, :], t["b_o2"].partition_broadcast(LANES))):
                sp.dma_start(dst, src).then_inc(s_ld, 16)
            sp.wait_ge(s_pool, 1)
            sp.dma_start(w_f1[0:R, :], t["w_f1T"]).then_inc(s_ld, 16)
            sp.dma_start(w_f1[R:R + 1, :], t["b_f1"]).then_inc(s_ld, 16)
            sp.dma_start(meta[:, SRC, :].bitcast(I32), t["src_col"]).then_inc(s_meta, 16)
            sp.dma_start(meta[:, WEIGHT, :], t["weight_col"]).then_inc(s_meta, 16)
            sp.wait_ge(s_dve, 1)
            sp.dma_start(seg_i[:, :], t["dst_seg"]).then_inc(s_seg, 16)
            sp.dma_start(ends16[0, :].rearrange("(p e) -> p e", e=SEG), seg_u[:, 0, :]).then_inc(s_e16, 16)
            sp.wait_ge(s_dve, 2)
            sp.dma_start(ends16[1, :].rearrange("(p e) -> p e", e=SEG), seg_u[:, 1, :]).then_inc(s_e16, 16)
            for k in range(2):
                sp.dma_start(win_dram[0, k, :].rearrange("(p e) -> p e", e=SEG_PAIRS), seg_win[:, k, :]).then_inc(s_win_st, 16)
            sp.wait_ge(s_win_st, 32)
            sp.dma_start(win_first[:, :, :], win_dram[:, :, :]).then_inc(s_win_ld, 16)
            sp.dma_start(win_i[:, :], win_dram[:, 0, :].partition_broadcast(LANES)).then_inc(s_win_ld, 16)
            sp.wait_ge(s_dve, 3)
            sp.wait_ge(s_pool, 2)
            for part in range(PARTS):
                for k in range(TILES_U):
                    sp.dma_start(b_f2_rows[part:part + 1, k, :], bias_part[0:1, part, 0, :]).then_inc(s_part, 16)
                sp.dma_start(b_o1_rows[part:part + 1, :], bias_part[0:1, part, 1, :]).then_inc(s_part, 16)

            def store_h(g, b):
                wait_for(sp, s_h2, g, 1, 1)
                sp.sem_inc(s_carry, 1)
                sp.dma_start(h3_view[:, bass.ds(g.value() * NODE_G, NODE_G), :],
                             h_parts[:, b, :, :, :].rearrange("p n s f -> p n (s f)")).then_inc(s_hst[b], 16)

            groups_loop(sp, store_h)
            sp.wait_ge(s_e16, 32)
            for b in range(2):
                sp.wait_ge(s_hst[b], 16 * (n_groups // 2))
            sp.wait_ge(s_pool, 3)
            sp.wait_ge(s_zero, 16 * TABLES)

            def phase_b(anywhere):
                def load_pair(p, q):
                    wait_for(sp, s_z, p, 2, -2)
                    sp.sem_inc(s_carry, 1)
                    sp.dma_start(attr[0:R, q, :], t["attrT"][:, bass.ds(p.value() * PAIR, PAIR)]).then_inc(s_attr[q], 16)
                    wait_for(sp, s_same, p, 2, -2)
                    sp.sem_inc(s_carry, 1)
                    sp.dma_start(ends[:, q, :, :],
                                 ends16[:, bass.ds(p.value() * PAIR, PAIR)].unsqueeze(0).to_broadcast([LANES, 2, PAIR])
                                 ).then_inc(s_ends[q], 16)
                    if anywhere:
                        wait_for(sp, s_win[q], p.halved(), 16 * TILES_P)
                        sp.sem_inc(s_carry, 1)
                        sp.dma_start(dst_p[:, q, :], t["dst_col"][:, bass.ds(p.value() * TILES_P, TILES_P)]).then_inc(s_dst[q], 16)
                    else:
                        first = sp.value_load(win_first[0:1, 0, bass.ds(p.value(), 1)], min_val=0, max_val=n_pad - WINDOW)
                        wait_for(sp, s_ph, p, 2, -2)
                        sp.sem_inc(s_carry, 1)
                        sp.dma_start(win[:, q, 0, :], h3[bass.ds(first, WINDOW), :]).then_inc(s_win[q], 16)

                for q in range(2):
                    load_pair(Count(q), q)
                with sp.Fori(1, n_iter) as i:
                    for q in range(2):
                        load_pair(Count(q, 2, i), q)

            either(sp, phase_b)

            for k in range(TABLES):
                sp.wait_ge(s_scat[k], 16 * n_units * TILES_U // TABLES)

            def node_loads(g, b):
                wait_for(sp, s_aT, g, 1, -1)
                sp.sem_inc(s_carry, 1)
                for k in range(TABLES // 2):
                    sp.dma_start(tab_in[:, b, k, :, :], tab_view[k][:, bass.ds(g.value() * NODE_G, NODE_G), :]).then_inc(s_tab[b], 16)

            def node_stores(g):
                wait_for(sp, s_of, g, 1, 2)
                sp.sem_inc(s_carry, 1)
                for lo, hi in lots:
                    sp.dma_start(out_rows[lo:hi, bass.ds(g.value() * NODE_G, 2 * NODE_G), :],
                                 x_all[lo:hi, bass.ds(g.value() * NODE_G, 2 * NODE_G), :]).then_inc(s_out, 16)

            for b in range(2):
                node_loads(Count(b), b)
            with sp.Fori(1, n_groups // 2) as i:
                for b in range(2):
                    node_loads(Count(b, 2, i), b)
                node_stores(Count(-2, 2, i))
            node_stores(Count(n_groups - 2))
            sp.dma_start(t["out"][full_lanes * rows_l:n_nodes, :].rearrange("(p n) f -> p n f", p=1),
                         x_all[full_lanes:full_lanes + 1, 0:last_rows, :]).then_inc(s_out, 16)
            sp.wait_ge(s_out, 16 * (len(lots) * n_groups // 2 + 1))

        @block.gpsimd
        def _(pool):
            pool.memset(w_f1[:, :], 0.0).then_inc(s_pool, 1)
            pool.memset(b_o1_rows[:, :], 0.0)
            pool.memset(b_f2_rows[:, :, :], 0.0).then_inc(s_pool, 1)
            pool.memset(attr[:, :, :], 1.0).then_inc(s_pool, 1)
            pool.memset(ones_bf[:, :], 1.0)
            pool.iota(lane[:, :], pattern=[[0, 1]], base=0, channel_multiplier=1,
                      allow_small_or_imprecise_dtypes=True)
            pool.memset(ident[:, :], 0.0)
            pool.memset(ident_bf[:, :], 0.0).then_inc(s_pool, 1)
            pool.wait_ge(s_pool, 4)
            for m in (ident, ident_bf):
                pool.affine_select(out=m[:, :], in_=m[:, :], compare_op=ALU.not_equal, fill=1.0, base=0,
                                   pattern=[[-1, LANES]], channel_multiplier=1).then_inc(s_pool, 1)
            pool.wait_ge(s_zero, 16 * TABLES)
            for b in range(2):
                pool.wait_ge(s_hst[b], 16 * (n_groups // 2))

            def phase_b(anywhere):
                def gather(p, q):
                    wait_for(pool, s_dst[q], p.halved(), 16, 16)
                    wait_for(pool, s_ph, p, 2, -2)
                    pool.sem_inc(s_go, 1)
                    for k in range(TILES_P):
                        pool.indirect_dma_start(out=win[:, q, k, :], out_offset=None, in_=h3[:, :],
                                                in_offset=bass.IndirectOffsetOnAxis(ap=dst_p[:, q, k:k + 1], axis=0),
                                                ).then_inc(s_win[q], 16)

                def scatter(p, q):
                    for v in range(UNITS_P):
                        wait_for(pool, s_idx, p, 2, v + 1)
                        wait_for(pool, s_ysb, p, 2, v + 1)
                        for k in range(v * TILES_U, (v + 1) * TILES_U):
                            if TABLES == TILES_P:
                                wait_for(pool, s_scat[k], p, 16)
                            else:
                                wait_for(pool, s_scat[k % TABLES], p, 32, 16 * v)
                            pool.sem_inc(s_rot if k % TILES_U == TILES_U - 1 else s_go, 1)
                            pool.indirect_dma_start(out=tables[k % TABLES][:, :],
                                                    out_offset=bass.IndirectOffsetOnAxis(ap=row_idx[:, q, k:k + 1], axis=0),
                                                    in_=y_sb[:, q, k, :], in_offset=None,
                                                    compute_op=ALU.add).then_inc(s_scat[k % TABLES], 16)

                if anywhere:
                    gather(Count(0), 0)
                    gather(Count(1), 1)
                scatter(Count(0), 0)
                with pool.Fori(1, n_iter) as i:
                    if anywhere:
                        gather(Count(0, 2, i), 0)
                    scatter(Count(-1, 2, i), 1)
                    if anywhere:
                        gather(Count(1, 2, i), 1)
                    scatter(Count(0, 2, i), 0)
                scatter(Count(n_pairs - 1), 1)

            either(pool, phase_b)
            for k in range(TABLES):
                pool.wait_ge(s_scat[k], 16 * n_units * TILES_U // TABLES)

            def node_loads(g, b):
                wait_for(pool, s_aT, g, 1, -1)
                pool.sem_inc(s_go, 1)
                for k in range(TABLES // 2, TABLES):
                    pool.dma_start(tab_in[:, b, k, :, :], tab_view[k][:, bass.ds(g.value() * NODE_G, NODE_G), :]).then_inc(s_tab2[b], 16)

            groups_loop(pool, node_loads)

        @block.scalar
        def _(act):
            act.wait_ge(s_xb, 2)
            zero_n = next(n for n in (11, 9, 7, 5, 3, 2, 1) if t_rows % n == 0)
            zeros = win[:, :, :, :].rearrange("p q k f -> p (q k f)").bitcast(F32)[:, 0:zero_n * F]
            for tb in tables:
                act.dma_start(tb[:, :].rearrange("(p a n) f -> p a (n f)", p=LANES, n=zero_n),
                              zeros.unsqueeze(1).to_broadcast([LANES, t_rows // zero_n, zero_n * F])).then_inc(s_zero, 16)
            act.wait_ge(s_mv, n_groups)
            act.wait_ge(s_pool, 6)
            act.activation(rstd[:, :], mean_var[:, :, 1], ACT.Sqrt, bias=eps[0:NODE_P, :]).then_inc(s_sqrt, 1)
            act.wait_ge(s_dve, 4)

            def normalize(g, b):
                wait_for(act, s_hT, g, 1, -1)
                for k in range(NODE_G):
                    n = bass.ds(g.value(NODE_G, k), 1)
                    last = act.activation(hn[:, b, k, :], x_all[:, n, :].rearrange("p a f -> p (a f)"),
                                          ACT.Relu, bias=shift[:, n], scale=rstd[:, n])
                last.then_inc(s_hn, 1)

            def first_part(g, b):
                wait_for(act, s_hm, g, 1, 1)
                wait_for(act, s_hst[b], g.halved(), 16)
                act.copy(h_parts[:, b, :, 0, :], p_w[b][0:NODE_P, :, :]).then_inc(s_h0, 1)

            def second_part(g, b):
                wait_for(act, s_hr, g, 1, 1)
                act.copy(h_parts[:, b, :, 1, :], h_rest[:, b, :, :]).then_inc(s_h1, 1)

            normalize(Count(0), 0)

            def phase_a(g, b, more=True):
                if more:
                    normalize(Count(g.base + 1, g.per_iter, g.i), 1 - b)
                first_part(g, b)
                second_part(g, b)

            phase_a(Count(0), 0)
            with act.Fori(1, n_groups // 2) as i:
                phase_a(Count(-1, 2, i), 1)
                phase_a(Count(0, 2, i), 0)
            phase_a(Count(n_groups - 1), 1, more=False)

            def gelu_of(n, v):
                wait_for(act, s_z, n, 1, 1)
                wait_for(act, s_smu, n, 1, -1)
                act.activation(gelu[:, v, :], p_z[:, :], ACT.Gelu, scale=SMU_S).then_inc(s_gelu, 1)

            def weigh(n, p, q, v):
                wait_for(act, s_ph, n, 1, 1)
                wait_for(act, s_metap, p, 1, 1)
                wait_for(act, s_msg, n, 1, -1)
                for k in range(TILES_U):
                    kk = v * TILES_U + k
                    last = act.activation(hg[:, v, k, :], p_h[:, k, :], ACT.Copy, scale=meta_p[:, q, WEIGHT, kk:kk + 1])
                last.then_inc(s_hg, 1)

            def rows_out(n, q, v):
                wait_for(act, s_idx, n, 1, 1)
                wait_for(act, s_rot, n, 1, -1)
                act.copy(y_sb[:, q, v * TILES_U:(v + 1) * TILES_U, :], p_y[v][:, :, 0:F]).then_inc(s_ysb, 1)

            def step(i, c, base):
                st = Step(i, c, base)
                if st.has(0):
                    gelu_of(st.unit(), st.v())
                if st.has(1):
                    weigh(st.unit(1), st.pair(1), st.q(1), st.v(1))
                if st.has(2):
                    rows_out(st.unit(2), st.q(2), st.v(2))

            edge_loop(act, step)

            def gelu_out(g, b):
                wait_for(act, s_u, g, 1, 1)
                wait_for(act, s_os, g, 1, -1)
                act.activation(attr[:, 0, b * BANK:b * BANK + GROUP], p_y[b][:, 2:4, :].rearrange("p a n -> p (a n)")[:, 0:GROUP],
                               ACT.Gelu, scale=SMU_S).then_inc(s_oe, 1)

            groups_loop(act, gelu_out)

        @block.vector
        def _(dve):
            n_red = [0]

            def link(ins):
                ins.then_inc(s_red, 1)
                n_red[0] += 1
                dve.wait_ge(s_red, n_red[0])

            dve.memset(x_all[full_lanes // 32 * 32:, last_rows:, :], 0.0).then_inc(s_xb, 1)
            dve.memset(win[:, :, :, :], 0.0).then_inc(s_xb, 1)
            dve.memset(eps[:, :], EPS)
            dve.wait_ge(s_x, 16 * 3)

            def node_stats(g, b):
                wait_for(dve, s_mv, g, 1, -1)
                for k in range(NODE_G):
                    last = dve.bn_stats(stats[:, b, k, :], x_all[:, bass.ds(g.value(NODE_G, k), 1), :].rearrange("p a f -> p (a f)"))
                last.then_inc(s_red, 1)
                wait_for(dve, s_red, g, 1, 1)
                dve.sem_inc(s_carry_v, 1)
                for k in range(NODE_G):
                    last = dve.bn_aggr(mean_var_g[:, b, k, :], stats[:, b, k, :])
                last.then_inc(s_add, 1)
                wait_for(dve, s_add, g, 1, 1)
                dve.tensor_copy(mean_var[:, bass.ds(g.value(NODE_G), NODE_G), :], mean_var_g[:, b, :, :]).then_inc(s_mv, 1)

            dve.wait_ge(s_seg, 16)
            dve.tensor_copy(seg_u[:, 0, :], seg_i[:, :]).then_inc(s_dve, 1)
            groups_loop(dve, node_stats)
            n_red[0] = n_groups
            dve.wait_ge(s_seg, 32)
            dve.tensor_copy(seg_u[:, 1, :], seg_i[:, :])
            pairs_of = seg_i[:, :].rearrange("p (a e) -> p a e", e=PAIR)
            dve.tensor_reduce(seg_min[:, 0, :], pairs_of, axis=AX.X, op=ALU.min)
            link(dve.tensor_reduce(seg_min[:, 1, :], pairs_of, axis=AX.X, op=ALU.max))
            link(dve.tensor_scalar(seg_min[:, 0, :], seg_min[:, 0, :], float(n_pad - WINDOW), None, ALU.min))
            link(dve.tensor_tensor(seg_min[:, 1, :], seg_min[:, 1, :], seg_min[:, 0, :], ALU.subtract))
            dve.tensor_copy(seg_win[:, :, :], seg_min[:, :, :]).then_inc(s_dve, 1)
            dve.wait_ge(s_ld, 16 * N_LD)
            for part in range(PARTS - 1):
                link(dve.tensor_copy(bias_part[0:1, part, :, :], bias[0:1, part, :, :]))
                link(dve.tensor_tensor(bias[0:1, part + 1, :, :], bias[0:1, part, :, :], bias_part[0:1, part, :, :], ALU.subtract))
            dve.tensor_copy(bias_part[0:1, PARTS - 1, :, :], bias[0:1, PARTS - 1, :, :]).then_inc(s_dve, 1)
            dve.wait_ge(s_mv, n_groups)
            dve.tensor_scalar(w_f2[:, :], w_f2[:, :], SMU_W, None, ALU.mult)
            dve.tensor_scalar(w_o2[:, :], w_o2[:, :], SMU_W, None, ALU.mult)
            dve.wait_ge(s_sqrt, 1)
            link(dve.reciprocal(rstd[:, :], rstd[:, :]))
            dve.scalar_tensor_tensor(shift[:, :], mean_var[:, :, 0], -1.0, rstd[:, :], ALU.mult, ALU.mult).then_inc(s_dve, 1)
            dve.wait_ge(s_pool, 6)
            link(dve.tensor_scalar(tie_limit[:, :].bitcast(I32), lane[:, :], -1.0, 190.0, ALU.mult, ALU.add))
            link(dve.tensor_scalar(tie_weight[:, :].bitcast(I32), tie_limit[:, :].bitcast(I32), 23, None,
                                   ALU.logical_shift_left))
            dve.tensor_scalar(tie_limit[:, :], tie_weight[:, :], 2.5, None, ALU.mult)
            dve.tensor_copy(msg[:, :, :, F].rearrange("p a b -> p (a b)"), tie_weight[:, :].to_broadcast([LANES, 2 * TILES_U]))
            link(dve.tensor_scalar(dump_row[:, :], lane[:, :], float(dump), None, ALU.add))

            def transposed(g, b):
                wait_for(dve, s_hT, g, 1, 1)
                wait_for(dve, s_hm, g, 1, -1)
                dve.tensor_copy(hT[:, b, :, :], p_y[b][:, 0:2, :].rearrange("p a (two n) -> p (a two) n", two=2)[:, :, 0:NODE_P]).then_inc(s_hTs, 1)

            def rest_of_h(g, b):
                wait_for(dve, s_h2, g, 1, -1)
                wait_for(dve, s_h0, g, 1, 1)
                dve.tensor_tensor(h_rest[:, b, :, :], p_w[b][0:NODE_P, :, :], h_parts[:, b, :, 0, :], ALU.subtract).then_inc(s_hr, 1)

            def third_part(g, b):
                wait_for(dve, s_h1, g, 1, 1)
                dve.tensor_tensor(h_parts[:, b, :, 2, :], h_rest[:, b, :, :], h_parts[:, b, :, 1, :], ALU.subtract).then_inc(s_h2, 1)

            def phase_a(g, b, more=True):
                if more:
                    transposed(Count(g.base + 1, g.per_iter, g.i), 1 - b)
                rest_of_h(g, b)
                third_part(g, b)

            transposed(Count(0), 0)
            phase_a(Count(0), 0)
            with dve.Fori(1, n_groups // 2) as i:
                phase_a(Count(-1, 2, i), 1)
                phase_a(Count(0, 2, i), 0)
            phase_a(Count(n_groups - 1), 1, more=False)
            dve.wait_ge(s_meta, 32)
            dve.tensor_copy(meta[:, SRC, :], meta[:, SRC, :].bitcast(I32))
            dve.wait_ge(s_win_ld, 32)
            dve.tensor_scalar(win_row[:, :], win_i[:, :], lane[:, :], None, ALU.add)
            link(dve.tensor_reduce(reach[:, :], win_first[:, 1, :], axis=AX.X, op=ALU.max))
            dve.tensor_scalar(general[:, :], reach[:, :], float(WINDOW) - 0.5, None, ALU.is_gt).then_inc(s_flag, 1)
            dve.wait_ge(s_e16, 32)
            dve.tensor_tensor(x_all[:, :, :], x_all[:, :, :],
                              b_o2[0:NODE_P, :].unsqueeze(1).to_broadcast([NODE_P, rows_l, F]), ALU.add).then_inc(s_dve, 1)
            dve.wait_ge(s_dve, 5)

            def phase_b(anywhere):
                def pair_meta(p, q):
                    wait_for(dve, s_idx, p, 2, -2)
                    tiles = bass.ds(p.value() * TILES_P, TILES_P)
                    dve.tensor_copy(meta_p[:, q, 0:2, :], meta[:, :, tiles])
                    dve.tensor_scalar(meta_p[:, q, DUMP, :], meta[:, SRC, tiles], -1.0, dump_row[:, :], ALU.mult, ALU.add
                                      ).then_inc(s_metap, 1)

                def smu(n, v):
                    wait_for(dve, s_gelu, n, 1, 1)
                    wait_for(dve, s_w, n, 1, -1)
                    dve.scalar_tensor_tensor(act1[:, v, :], p_z[:, :], SMU_L, gelu[:, v, :], ALU.mult, ALU.add).then_inc(s_smu, 1)

                def message(n, v):
                    wait_for(dve, s_hg, n, 1, 1)
                    wait_for(dve, s_w, n, 1, 1)
                    wait_for(dve, s_y, n, 1, -1)
                    dve.tensor_tensor(msg[:, v, :, 0:F], p_w[v][:, :, :], hg[:, v, :, :], ALU.mult).then_inc(s_msg, 1)

                def row_numbers(n, q, v):
                    cols = slice(v * TILES_U, (v + 1) * TILES_U)
                    wait_for(dve, s_y, n, 1, 1)
                    wait_for(dve, s_rot, n, 1, -1)
                    dve.scalar_tensor_tensor(redirect[:, v, :], p_y[v][:, :, F], tie_limit[:, :], meta_p[:, q, DUMP, cols],
                                             ALU.is_gt, ALU.mult).then_inc(s_tie, 1)
                    wait_for(dve, s_tie, n, 1, 1)
                    dve.tensor_tensor(row_idx[:, q, cols], redirect[:, v, :], meta_p[:, q, SRC, cols], ALU.add).then_inc(s_idx, 1)

                def pick_target(n, p, q, v):
                    wait_for(dve, s_ph, n, 1, -1)
                    dve.tensor_scalar(pick[:, v, :], ends[:, q, 1, v * UNIT:(v + 1) * UNIT], win_row[:, bass.ds(p.value(), 1)], None,
                                      ALU.is_equal).then_inc(s_pick, 1)

                def same_source(n, q, v):
                    wait_for(dve, s_y, n, 1, -1)
                    dve.tensor_tensor(same[:, v, :, :],
                                      ends[:, q, 0, v * UNIT:(v + 1) * UNIT].rearrange("p (k e) -> p k e", k=TILES_U),
                                      meta_p[:, q, SRC, v * TILES_U:(v + 1) * TILES_U].unsqueeze(2).to_broadcast([LANES, TILES_U, LANES]),
                                      ALU.is_equal).then_inc(s_same, 1)

                def step(i, c, base):
                    st = Step(i, c, base)
                    if st.has(0) and c % 2 == 0:
                        pair_meta(st.pair(), st.q())
                        wait_for(dve, s_ends[st.q()], st.pair().halved(), 16, 16)
                        wait_for(dve, s_metap, st.pair(), 1, 1)
                    if st.has(0):
                        smu(st.unit(), st.v())
                        if not anywhere:
                            pick_target(st.unit(), st.pair(), st.q(), st.v())
                    if st.has(1):
                        message(st.unit(1), st.v(1))
                    if st.has(2):
                        row_numbers(st.unit(2), st.q(2), st.v(2))
                    if st.has(0):
                        same_source(st.unit(), st.q(), st.v())

                edge_loop(dve, step)

            either(dve, phase_b)

            def sum_tables(g, b):
                for loads in (s_tab, s_tab2):
                    wait_for(dve, loads[b], g.halved(), 8 * TABLES, 8 * TABLES)
                for k in range(1, DVE_TABLES):
                    dve.tensor_tensor(tab_in[:, b, 0, :, :], tab_in[:, b, 0, :, :], tab_in[:, b, k, :, :], ALU.add).then_inc(s_sum, 1)
                    wait_for(dve, s_sum, g, DVE_TABLES - 1, k)

            def sums_out(g, b):
                wait_for(dve, s_aT, g, 1, 1)
                wait_for(dve, s_u, g, 1, -1)
                dve.tensor_copy(hT[:, b, :, :], p_w[b][:, :, 0:NODE_P]).then_inc(s_aTs, 1)

            def smu_out(g, b):
                wait_for(dve, s_oe, g, 1, 1)
                wait_for(dve, s_om, g, 1, -1)
                dve.scalar_tensor_tensor(attr[:, 1, b * BANK:b * BANK + GROUP],
                                         p_y[b][:, 2:4, :].rearrange("p a n -> p (a n)")[:, 0:GROUP], SMU_L,
                                         attr[:, 0, b * BANK:b * BANK + GROUP], ALU.mult, ALU.add).then_inc(s_os, 1)

            def output(g, b):
                wait_for(dve, s_om, g, 1, 1)
                rows = bass.ds(g.value() * NODE_G, NODE_G)
                dve.tensor_tensor(x_all[:, rows, :], p_y[b][0:NODE_P, 0:2, :].rearrange("p a (two n) -> p (a two) n", two=2),
                                  x_all[:, rows, :], ALU.add).then_inc(s_of, 1)

            def phase_c(g, b, more=True):
                nxt = Count(g.base + 1, g.per_iter, g.i)
                sums_out(g, b)
                if more:
                    sum_tables(nxt, 1 - b)
                smu_out(g, b)
                output(g, b)

            sum_tables(Count(0), 0)
            phase_c(Count(0), 0)
            with dve.Fori(1, n_groups // 2) as i:
                phase_c(Count(-1, 2, i), 1)
                phase_c(Count(0, 2, i), 0)
            phase_c(Count(n_groups - 1), 1, more=False)

        @block.tensor
        def _(pe):
            pe.wait_ge(s_ld, 16 * N_LD)
            pe.wait_ge(s_pool, 6)

            def transpose_nodes(g, b):
                wait_for(pe, s_hn, g, 1, 1)
                wait_for(pe, s_hTs, g, 1, -1)
                for k in range(NODE_G):
                    last = pe.transpose(p_y[b][:, k // 2, k % 2 * LANES:k % 2 * LANES + NODE_P], hn[:, b, k, :],
                                        ident[0:NODE_P, 0:NODE_P])
                last.then_inc(s_hT, 1)

            def first_layer(g, b):
                wait_for(pe, s_hTs, g, 1, 1)
                wait_for(pe, s_hr, g, 1, -1)
                for k in range(NODE_G):
                    last = pe.matmul(p_w[b][0:NODE_P, k, :], hT[:, b, k, :], w_in[:, :], start=True, stop=True)
                last.then_inc(s_hm, 1)

            def phase_a(g, b, more=True):
                if more:
                    transpose_nodes(Count(g.base + 1, g.per_iter, g.i), 1 - b)
                first_layer(g, b)

            transpose_nodes(Count(0), 0)
            phase_a(Count(0), 0)
            with pe.Fori(1, n_groups // 2) as i:
                phase_a(Count(-1, 2, i), 1)
                phase_a(Count(0, 2, i), 0)
            phase_a(Count(n_groups - 1), 1, more=False)
            pe.wait_ge(s_h2, n_groups)
            pe.wait_ge(s_dve, 5)
            pe.wait_ge(s_part, 16 * PARTS * (TILES_U + 1))

            def phase_b(anywhere):
                def filter2(n, v):
                    wait_for(pe, s_smu, n, 1, 1)
                    wait_for(pe, s_msg, n, 1, -1)
                    pe.matmul(p_w[v][:, :, :], ones_bf[:, 0:LANES], b_f2_rows[:, :, :], start=True, stop=False)
                    for k in range(TILES_U):
                        last = pe.matmul(p_w[v][:, k, :], act1[:, v, k * LANES:(k + 1) * LANES], w_f2[:, :],
                                         start=False, stop=(k == TILES_U - 1))
                    last.then_inc(s_w, 1)

                def filter1(n, p, q, v):
                    if v == 0:
                        wait_for(pe, s_attr[q], p.halved(), 16, 16)
                    wait_for(pe, s_smu, n)
                    pe.matmul(p_z[:, :], w_f1[:, :], attr[:, q, v * UNIT:(v + 1) * UNIT], start=True, stop=True).then_inc(s_z, 1)

                def targets(n, p, q, v):
                    if v == 0:
                        count = 16 * TILES_P if anywhere else 16
                        wait_for(pe, s_win[q], p.halved(), count, count)
                    if not anywhere:
                        wait_for(pe, s_pick, n, 1, 1)
                    wait_for(pe, s_hg, n)
                    for k in range(TILES_U):
                        which = ident_bf[:, :] if anywhere else pick[:, v, k * LANES:(k + 1) * LANES]
                        for part in range(PARTS):
                            rows = win[:, q, v * TILES_U + k if anywhere else 0, part * F:(part + 1) * F]
                            last = pe.matmul(p_h[:, k, :], which, rows, start=(part == 0), stop=(part == PARTS - 1))
                    last.then_inc(s_ph, 1)

                def sum_same(n, v):
                    wait_for(pe, s_msg, n, 1, 1)
                    wait_for(pe, s_same, n, 1, 1)
                    wait_for(pe, s_ysb, n, 1, -1)
                    for k in range(TILES_U):
                        last = pe.matmul(p_y[v][:, k, 0:FT], same[:, v, k, :], msg[:, v, k, :], start=True, stop=True)
                    last.then_inc(s_y, 1)

                def step(i, c, base):
                    st = Step(i, c, base)
                    if st.has(1):
                        filter2(st.unit(1), st.v(1))
                    if st.has(0):
                        filter1(st.unit(), st.pair(), st.q(), st.v())
                    if st.has(1):
                        targets(st.unit(1), st.pair(1), st.q(1), st.v(1))
                    if st.has(2):
                        sum_same(st.unit(2), st.v(2))

                edge_loop(pe, step)

            either(pe, phase_b)

            pe.wait_ge(s_ysb, n_units)

            def transpose_sums(g, b):
                for loads in (s_tab, s_tab2):
                    wait_for(pe, loads[b], g.halved(), 8 * TABLES, 8 * TABLES)
                wait_for(pe, s_sum, g, DVE_TABLES - 1, DVE_TABLES - 1)
                wait_for(pe, s_aTs, g, 1, -1)
                left = [0] + list(range(DVE_TABLES, TABLES))
                for k in range(NODE_G):
                    for n, j in enumerate(left):
                        last = pe.matmul(p_w[b][:, k, 0:NODE_P], tab_in[:, b, j, k, :], ident[0:NODE_P, 0:NODE_P],
                                         start=(n == 0), stop=(n == len(left) - 1))
                last.then_inc(s_aT, 1)

            def hidden(g, b):
                wait_for(pe, s_aTs, g, 1, 1)
                wait_for(pe, s_os, g, 1, -1)
                out = p_y[b][:, 2:4, :].rearrange("p a n -> p (a n)")[:, 0:GROUP]
                pe.matmul(out, b_o1_rows[:, :], ones_bf[:, 0:GROUP], start=True, stop=False)
                pe.matmul(out, w_o1[:, :], hT[:, b, :, :], start=False, stop=True).then_inc(s_u, 1)

            def last_layer(g, b):
                wait_for(pe, s_os, g, 1, 1)
                wait_for(pe, s_of, g, 1, -1)
                for k in range(NODE_G):
                    last = pe.matmul(p_y[b][0:NODE_P, k // 2, k % 2 * LANES:k % 2 * LANES + F],
                                     attr[:, 1, b * BANK + k * NODE_P:b * BANK + (k + 1) * NODE_P], w_o2[:, :], start=True, stop=True)
                last.then_inc(s_om, 1)

            def phase_c(g, b, more=True):
                hidden(g, b)
                if more:
                    transpose_sums(Count(g.base + 1, g.per_iter, g.i), 1 - b)
                last_layer(g, b)

            transpose_sums(Count(0), 0)
            phase_c(Count(0), 0)
            with pe.Fori(1, n_groups // 2) as i:
                phase_c(Count(-1, 2, i), 1)
                phase_c(Count(0, 2, i), 0)
            phase_c(Count(n_groups - 1), 1, more=False)


def kernel(**inputs):
    import concourse.bacc as bacc
    from concourse.bass_utils import run_bass_kernel_spmd as run

    x = np.asarray(inputs["x"])
    n_nodes, F = x.shape
    attr = np.asarray(inputs["edge_attr_20"])
    n_edges, R = attr.shape
    padded = -(-n_edges // (BODY * UNIT)) * (BODY * UNIT)

    def pad(a):
        out = np.zeros((padded,) + a.shape[1:], a.dtype)
        out[:n_edges] = a
        return out

    def col(a):
        return np.ascontiguousarray(a.reshape(-1, LANES).T)

    src, dst = pad(np.asarray(inputs["src"])), pad(np.asarray(inputs["dst"]))
    dst[n_edges:] = dst[n_edges - 1]
    g = {k[len("L0_gnn_"):]: np.asarray(v) for k, v in inputs.items() if k.startswith("L0_gnn_")}
    arrays = {
        "x": np.ascontiguousarray(x),
        "attrT": np.ascontiguousarray(pad(attr).T),
        "src_seg": src.reshape(-1, 4 * PAIR),
        "dst_seg": dst.reshape(-1, 4 * PAIR),
        "src_col": col(src),
        "dst_col": col(dst),
        "weight_col": col(pad(np.asarray(inputs["edge_weight"]))),
        "w_inT": np.ascontiguousarray(g["W_in2f"].T),
        "w_f1T": np.ascontiguousarray(g["W_f1"].T),
        "w_f2T": np.ascontiguousarray(g["W_f2"].T),
        "w_o1T": np.ascontiguousarray(g["W_o1"].T),
        "w_o2T": np.ascontiguousarray(g["W_o2"].T),
        "b_f1": g["b_f1"].reshape(1, F),
        "bias2": np.concatenate([g["b_f2"], g["b_o1"]]).reshape(1, 2, F),
        "b_o2": g["b_o2"].reshape(1, F),
    }
    nc = bacc.Bacc("TRN2", target_bir_lowering=False, num_devices=1)
    t = {k: nc.dram_tensor(f"in_{k}", a.shape, mybir.dt.from_np(a.dtype), kind="ExternalInput").ap()
         for k, a in arrays.items()}
    t["out"] = nc.dram_tensor("out", (n_nodes, F), F32, kind="ExternalOutput").ap()
    build(nc, n_nodes, padded, F, R, t)
    r = run(nc, [{f"in_{k}": a for k, a in arrays.items()}], core_ids=[0])
    return r.results[0]["out"]
```

```python
import numpy as np
import concourse.bass as bass
from concourse import mybir
from contextlib import ExitStack

F32, BF16, I32, U16 = mybir.dt.float32, mybir.dt.bfloat16, mybir.dt.int32, mybir.dt.uint16
ALU = mybir.AluOpType
ACT = mybir.ActivationFunctionType
AX = mybir.AxisListType

LANES = 128
TILES_U = 4
UNIT = LANES * TILES_U
UNITS_P = 2
PAIR = UNIT * UNITS_P
TILES_P = TILES_U * UNITS_P
BODY = 4
DEEP = 4
TABLES = 6
FIRST_TABLES = 4
AHEAD_TABLES = 2
PARTS = 3
WINDOW = LANES
BANK = 512
NODE_P = 112
NODE_G = 4
GROUP = NODE_G * NODE_P
STATS_G = 8
SMU_S = 2.5 * 0.99 * 2 ** 0.5
SMU_W = 0.99 / SMU_S
SMU_L = 0.01 / SMU_W
EPS = 1e-5


class Count:

    def __init__(self, base, per_iter=0, i=None):
        self.base, self.per_iter, self.i = base, per_iter, i

    def value(self, times=1, plus=0):
        fixed = self.base * times + plus
        return fixed if self.i is None else self.i * (self.per_iter * times) + fixed

    def over(self, ways):
        return Count(self.base // ways, self.per_iter // ways, self.i)


def wait_for(eng, sem, at, times=1, plus=0):
    v = at.value(times, plus)
    if at.i is None and v <= 0:
        return
    eng.wait_ge(sem, v)


def build(nc, n_nodes, n_edges, n_real, F, R, t):
    n_units = n_edges // UNIT
    n_pairs = n_units // UNITS_P
    n_tiles = n_edges // LANES
    n_iter = n_units // BODY
    rows_l = -(-n_nodes // (NODE_P * BODY * NODE_G)) * BODY * NODE_G
    n_groups = rows_l // NODE_G
    n_pad = NODE_P * rows_l
    full_lanes, last_rows = divmod(n_nodes, rows_l)
    spray = full_lanes // 16 * 16
    t_rows = rows_l + -(-LANES // NODE_P)
    dump = n_pad
    zero_n = next(n for n in range(min((2 * TILES_P - 2) * PARTS // 2, DEEP * NODE_G * PARTS // 2), 0, -1) if t_rows % n == 0)
    zero_parts = t_rows // zero_n
    late_passes = zero_parts * (TABLES - FIRST_TABLES) // 2
    pass_pairs = int(np.lcm(2, TABLES // np.gcd(TABLES, TILES_P)))
    scattered = n_pairs - 1 if (n_pairs - 1) * PAIR >= n_real else n_pairs
    few_pairs = next(n for n in range(2 * late_passes + 3, n_pairs, 2) if (n_pairs - 1 - n) % pass_pairs == 0)
    DVE_TABLES = TABLES - 1
    SEG_PAIRS = 4
    seg_lanes = n_pairs // SEG_PAIRS
    SEG = SEG_PAIRS * PAIR

    h3 = nc.dram_tensor("h3", [n_pad, PARTS * F], BF16, kind="Internal")
    tables = [nc.dram_tensor(f"sum_table{k}", [t_rows * NODE_P, F], F32, kind="Internal") for k in range(TABLES)]
    ends16 = nc.dram_tensor("ends16", [2, n_edges], U16, kind="Internal")
    win_dram = nc.dram_tensor("win_dram", [1, 2, n_pairs], I32, kind="Internal")

    ctx = ExitStack()
    with ctx:
        def sb(name, shape, dt=F32, stack=ctx):
            return stack.enter_context(nc.sbuf_tensor(name, shape, dt))

        def ps(name, shape, dt=F32):
            return ctx.enter_context(nc.psum_tensor(name, shape, dt))

        def sem(name):
            return ctx.enter_context(nc.semaphore(name))

        ident = sb("ident", [LANES, LANES])
        ident_bf = sb("ident_bf", [LANES, LANES], BF16)
        ones_bf = sb("ones_bf", [LANES, BANK], BF16)
        tie_weight = sb("tie_weight", [LANES, 1])
        tie_limit = sb("tie_limit", [LANES, 1])
        lane = sb("lane", [LANES, 1])
        dump_row = sb("dump_row", [LANES, 1])
        eps = sb("eps", [LANES, 1])
        w_in = sb("w_in", [F, F])
        w_f1 = sb("w_f1", [LANES, F])
        w_f2 = sb("w_f2", [F, F])
        w_o1 = sb("w_o1", [F, F])
        w_o2 = sb("w_o2", [F, F])
        B_F2, B_O1, B_O2, BIASES = 0, 1, 2, 3
        bias = sb("bias", [1, PARTS, BIASES, F])
        bias_part = sb("bias_part", [1, PARTS, BIASES, F], BF16)
        bias_rows = sb("bias_rows", [LANES, BIASES, TILES_U, F], BF16)
        x_all = sb("x_all", [NODE_P, rows_l, F])
        mean_var = sb("mean_var", [NODE_P, rows_l, 2])
        stats = sb("stats", [NODE_P, 2, STATS_G, 6])
        mean_var_g = sb("mean_var_g", [NODE_P, 2, STATS_G, 2])
        rstd = sb("rstd", [NODE_P, rows_l])
        shift = sb("shift", [NODE_P, rows_l])
        hn = sb("hn", [NODE_P, 2, NODE_G, F])
        hT = sb("hT", [F, 2, NODE_G, NODE_P])
        h_rest = sb("h_rest", [NODE_P, 2, NODE_G, F])
        h_parts = sb("h_parts", [NODE_P, DEEP, NODE_G, PARTS, F], BF16)
        win_first = sb("win_first", [1, 2, n_pairs], I32)
        win_row = sb("win_row", [LANES, n_pairs])
        win_i = sb("win_i", [LANES, n_pairs], I32)
        reach = sb("reach", [1, 1])
        general = sb("general", [1, 1], I32)
        seg_min = sb("seg_min", [seg_lanes, 2, SEG_PAIRS])
        seg_win = sb("seg_win", [seg_lanes, 2, SEG_PAIRS], I32)
        SRC, WEIGHT, DUMP = 0, 1, 2
        meta_p = sb("meta_p", [LANES, 2, 3, TILES_P])
        dst_p = sb("dst_p", [LANES, 2, TILES_P], I32)
        row_idx = sb("row_idx", [LANES, 2, TILES_P], I32)
        redirect = sb("redirect", [LANES, 2, TILES_U])
        attr = sb("attr", [LANES, 2, PAIR])
        FT = F + 1
        msg = sb("msg", [LANES, 2, TILES_U, FT])
        with ExitStack() as phase_c_only:
            tab_in = sb("tab_in", [NODE_P, DEEP, TABLES, NODE_G, F], F32, phase_c_only)
        meta = sb("meta", [LANES, 2, n_tiles])
        win = sb("win", [LANES, 2, TILES_P, PARTS * F], BF16)
        with ExitStack() as ahead_only:
            seg_i = sb("seg_i", [seg_lanes, 2, SEG], I32, ahead_only)
            seg_u = sb("seg_u", [seg_lanes, 2, SEG], U16, ahead_only)
        ends = sb("ends", [LANES, 2, 2, PAIR], U16)
        y_sb = sb("y_sb", [LANES, 2, TILES_P, F])
        gelu = sb("gelu", [F, 2, UNIT])
        act1 = sb("act1", [F, 2, UNIT])
        same = sb("same", [LANES, 2, TILES_U, LANES])
        pick = sb("pick", [LANES, 2, UNIT], BF16)
        hg = sb("hg", [LANES, 2, TILES_U, F])

        p_z = ps("p_z", [LANES, BANK])
        p_w = [ps(f"p_w{v}", [LANES, TILES_U, F]) for v in range(2)]
        p_h = ps("p_h", [LANES, TILES_U, F])
        p_y = [ps(f"p_y{v}", [LANES, TILES_U, BANK // 2]) for v in range(2)]

        s_x = sem("s_x")
        s_ld = sem("s_ld")
        s_seg = [sem(f"s_seg{e}") for e in range(2)]
        s_meta = sem("s_meta")
        s_zero = [sem(f"s_zero{k}") for k in range(TABLES)]
        s_pool = sem("s_pool")
        s_u16 = sem("s_u16")
        s_zeros = sem("s_zeros")
        s_seg_win = sem("s_seg_win")
        s_parts = sem("s_parts")
        s_shift = sem("s_shift")
        s_scaled = sem("s_scaled")
        s_red = sem("s_red")
        s_moved = sem("s_moved")
        s_st, s_ag, s_mv = sem("s_st"), sem("s_ag"), sem("s_mv")
        s_sqrt = sem("s_sqrt")
        s_carry_v = sem("s_carry_v")
        s_carry_a = sem("s_carry_a")
        s_carry = sem("s_carry")
        s_e16 = sem("s_e16")
        s_win_st, s_win_ld = sem("s_win_st"), sem("s_win_ld")
        s_flag = sem("s_flag")
        s_hn, s_hT, s_hTs, s_hm, s_h0, s_hr, s_h1, s_h2 = (
            sem(n) for n in ("s_hn", "s_hT", "s_hTs", "s_hm", "s_h0", "s_hr", "s_h1", "s_h2"))
        s_hst = [sem(f"s_hst{b}") for b in range(DEEP)]
        s_attr = [sem(f"s_attr{q}") for q in range(2)]
        s_ends = [sem(f"s_ends{q}") for q in range(2)]
        s_win = [sem(f"s_win{q}") for q in range(2)]
        s_dst = [sem(f"s_dst{q}") for q in range(2)]
        s_scat = [sem(f"s_scat{k}") for k in range(TABLES)]
        s_z, s_gelu, s_smu, s_w, s_pick, s_ph, s_hg, s_msg, s_same, s_y, s_idx, s_ysb, s_rot = (
            sem(n) for n in ("s_z", "s_gelu", "s_smu", "s_w", "s_pick", "s_ph", "s_hg", "s_msg", "s_same", "s_y",
                             "s_idx", "s_ysb", "s_rot"))
        s_metap = sem("s_metap")
        s_tie = sem("s_tie")
        s_go = sem("s_go")
        s_tab = [sem(f"s_tab{b}") for b in range(DEEP)]
        s_tab2 = [sem(f"s_tab2{b}") for b in range(DEEP)]
        s_out = sem("s_out")
        s_sum, s_aT, s_aTs, s_u, s_oe, s_os, s_om, s_of = (
            sem(n) for n in ("s_sum", "s_aT", "s_aTs", "s_u", "s_oe", "s_os", "s_om", "s_of"))

        N_LD = 7
        late_zeros = h_parts[:, :, :, :, :].rearrange("p d n s f -> p (d n s f)").bitcast(F32)[:, 0:zero_n * F].rearrange(
            "p (n f) -> p n f", f=F)
        window_slot = [0, TILES_P - 1]
        first_adds = [few_pairs * TILES_P // FIRST_TABLES if k < FIRST_TABLES else 0 for k in range(TABLES)]
        adds_to = [first_adds[k] + ((scattered - few_pairs) * TILES_P - k - 1) // TABLES + 1 for k in range(TABLES)]
        x_rows = t["x"][0:full_lanes * rows_l, :].rearrange("(p n) f -> p n f", n=rows_l)
        out_rows = t["out"][0:full_lanes * rows_l, :].rearrange("(p n) f -> p n f", n=rows_l)
        h3_view = h3[:, :].rearrange("(p n) f -> p n f", p=NODE_P)
        tab_view = [tb[0:n_pad, :].rearrange("(p n) f -> p n f", p=NODE_P) for tb in tables]
        lots = [(0, spray), (spray, full_lanes)]

        def loop(eng, step, n, lag, body=BODY):
            peeled = 1 if lag + 1 < body else 2
            for c in range(body * peeled):
                step(Step(None, c, 0, n, body))
            with eng.Fori(peeled, n // body) as i:
                for c in range(body):
                    step(Step(i, c, 0, n, body))
            for c in range(lag):
                step(Step(None, c, n, n, body))

        class Step:

            def __init__(self, i, c, base, n, body):
                self.i, self.c, self.base, self.n, self.body = i, c, base, n, body

            def has(self, back):
                return self.i is not None or 0 <= self.base + self.c - back < self.n

            def at(self, back=0):
                return Count(self.base + self.c - back, self.body if self.i is not None else 0, self.i)

            def pair(self, back=0):
                return Count((self.base + self.c - back) // 2, 2 if self.i is not None else 0, self.i)

            def q(self, back=0):
                return (self.c - back) // 2 % 2

            def v(self, back=0):
                return (self.c - back) % 2

            def deep(self, back=0):
                return (self.c - back) % DEEP

        block = ctx.enter_context(nc.Block())

        def either(eng, program):
            eng.wait_ge(s_flag, 1)
            anywhere = eng.value_load(general[0:1, 0:1], min_val=0, max_val=1)
            with eng.If(anywhere):
                program(True)
            with eng.Else():
                program(False)

        @block.sync
        def _(sp):
            for n_lot, (lo, hi) in enumerate(lots):
                if n_lot == 1:
                    sp.wait_ge(s_zeros, 1)
                sp.dma_start(x_all[lo:hi, :, :], x_rows[lo:hi, :, :]).then_inc(s_x, 16)
            sp.dma_start(x_all[full_lanes:full_lanes + 1, 0:last_rows, :],
                         t["x"][full_lanes * rows_l:n_nodes, :].rearrange("(p n) f -> p n f", p=1)).then_inc(s_x, 16)
            for dst, src in ((w_in[:, :], t["w_inT"]), (w_f2[:, :], t["w_f2T"]),
                             (w_o1[:, :], t["w_o1T"]), (w_o2[:, :], t["w_o2T"]),
                             (bias[0:1, 0, :, :], t["biases"])):
                sp.dma_start(dst, src).then_inc(s_ld, 16)
            sp.wait_ge(s_pool, 1)
            sp.dma_start(w_f1[0:R, :], t["w_f1T"]).then_inc(s_ld, 16)
            sp.dma_start(w_f1[R:R + 1, :], t["b_f1"]).then_inc(s_ld, 16)
            sp.wait_ge(s_seg_win, 1)
            for k in range(2):
                sp.dma_start(win_dram[0, k, :].rearrange("(p e) -> p e", e=SEG_PAIRS), seg_win[:, k, :]).then_inc(s_win_st, 16)
            sp.wait_ge(s_win_st, 32)
            sp.dma_start(win_first[:, :, :], win_dram[:, :, :]).then_inc(s_win_ld, 16)
            sp.dma_start(win_i[:, :], win_dram[:, 0, :].partition_broadcast(LANES)).then_inc(s_win_ld, 16)
            sp.wait_ge(s_parts, 1)
            sp.wait_ge(s_pool, 2)
            for part in range(PARTS):
                for one in range(BIASES):
                    sp.dma_start(bias_rows[part:part + 1, one, :, :],
                                 bias_part[0:1, part, one, :].unsqueeze(1).to_broadcast([1, TILES_U, F])).then_inc(s_moved, 16)
            for e in range(2):
                sp.wait_ge(s_u16, e + 1)
                sp.dma_start(ends16[e, :].rearrange("(p e) -> p e", e=SEG), seg_u[:, e, :]).then_inc(s_e16, 16)

            def store_h(st):
                wait_for(sp, s_h2, st.at(), 1, 1)
                sp.sem_inc(s_carry, 1)
                sp.dma_start(h3_view[:, bass.ds(st.at().value() * NODE_G, NODE_G), :],
                             h_parts[:, st.deep(), :, :, :].rearrange("p n s f -> p n (s f)")).then_inc(s_hst[st.deep()], 16)

            loop(sp, store_h, n_groups, 0)
            sp.wait_ge(s_e16, 32)
            sp.wait_ge(s_pool, 6)

            def phase_b(anywhere):
                def load_pair(p, q):
                    wait_for(sp, s_z, p, 2, -2)
                    sp.sem_inc(s_carry, 1)
                    sp.dma_start(attr[0:R, q, :], t["attrT"][:, bass.ds(p.value() * PAIR, PAIR)]).then_inc(s_attr[q], 16)
                    wait_for(sp, s_same, p, 2, -2)
                    sp.sem_inc(s_carry, 1)
                    sp.dma_start(ends[:, q, :, :],
                                 ends16[:, bass.ds(p.value() * PAIR, PAIR)].unsqueeze(0).to_broadcast([LANES, 2, PAIR])
                                 ).then_inc(s_ends[q], 16)
                    if anywhere:
                        wait_for(sp, s_win[q], p.over(2), 16 * TILES_P)
                        sp.sem_inc(s_carry, 1)
                        sp.dma_start(dst_p[:, q, :], t["dst_col"][:, bass.ds(p.value() * TILES_P, TILES_P)]).then_inc(s_dst[q], 16)
                    else:
                        first = sp.value_load(win_first[0:1, 0, bass.ds(p.value(), 1)], min_val=0, max_val=n_pad - WINDOW)
                        if p.i is None:
                            for b in range(DEEP):
                                sp.wait_ge(s_hst[b], 16 * (n_groups // DEEP))
                        wait_for(sp, s_ph, p, 2, -2)
                        sp.sem_inc(s_carry, 1)
                        sp.dma_start(win[:, q, window_slot[q], :], h3[bass.ds(first, WINDOW), :]).then_inc(s_win[q], 16)

                for q in range(2):
                    load_pair(Count(q), q)
                sp.wait_ge(s_pool, 7)
                ends_of = [1 + n * zero_parts for n in range((TABLES - FIRST_TABLES) // 2 + 1)] + [n_iter]
                for n, (lo, hi) in enumerate(zip(ends_of, ends_of[1:])):
                    with sp.Fori(lo, hi) as i:
                        for q in range(2):
                            load_pair(Count(q, 2, i), q)
                            k = FIRST_TABLES + 2 * n + q
                            if k < TABLES:
                                part = bass.ds((i - lo) * zero_n, zero_n)
                                sp.dma_start(tables[k][:, :].rearrange("(p n) f -> p n f", p=NODE_P)[:, part, :], late_zeros
                                             ).then_inc(s_zero[k], 16)

            either(sp, phase_b)

            sp.wait_ge(s_ysb, n_units)
            for k in range(TABLES):
                sp.wait_ge(s_scat[k], 16 * adds_to[k])

            def node_loads(st):
                wait_for(sp, s_aT, st.at(), 1, 1 - DEEP)
                sp.sem_inc(s_carry, 1)
                for k in range(TABLES // 2):
                    sp.dma_start(tab_in[:, st.deep(), k, :, :],
                                 tab_view[k][:, bass.ds(st.at().value() * NODE_G, NODE_G), :]).then_inc(s_tab[st.deep()], 16)

            loop(sp, node_loads, n_groups, 0)
            sp.wait_ge(s_out, 16 * (len(lots) * n_groups // 2 + 1))

        @block.gpsimd
        def _(pool):
            pool.memset(w_f1[:, :], 0.0).then_inc(s_pool, 1)
            pool.memset(bias_rows[:, :, :, :], 0.0).then_inc(s_pool, 1)
            pool.memset(ones_bf[:, :], 1.0)
            pool.iota(lane[:, :], pattern=[[0, 1]], base=0, channel_multiplier=1,
                      allow_small_or_imprecise_dtypes=True)
            pool.memset(ident[:, :], 0.0)
            pool.memset(ident_bf[:, :], 0.0).then_inc(s_pool, 1)
            pool.wait_ge(s_pool, 3)
            for m in (ident, ident_bf):
                pool.affine_select(out=m[:, :], in_=m[:, :], compare_op=ALU.not_equal, fill=1.0, base=0,
                                   pattern=[[-1, LANES]], channel_multiplier=1).then_inc(s_pool, 1)
            zeros = win[0:NODE_P, :, :, :].rearrange("p q k f -> p (q k f)").bitcast(F32)[:, PARTS * F // 2:PARTS * F // 2 + zero_n * F]
            pool.wait_ge(s_zeros, 2)
            pool.wait_ge(s_x, 16 * 3)
            for k, tb in enumerate(tables[:AHEAD_TABLES]):
                pool.dma_start(tb[:, :].rearrange("(p a n) f -> p a (n f)", p=NODE_P, n=zero_n),
                               zeros.unsqueeze(1).to_broadcast([NODE_P, t_rows // zero_n, zero_n * F])).then_inc(s_zero[k], 16)
            for e in range(2):
                pool.wait_ge(s_seg[e], 16)
                pool.tensor_copy(seg_u[:, e, :], seg_i[:, e, :]).then_inc(s_u16, 1)
            pool.memset(attr[:, :, :], 1.0).then_inc(s_pool, 1)
            beside = range(AHEAD_TABLES, FIRST_TABLES)
            with pool.Fori(0, zero_parts) as part:
                for n, k in enumerate(beside):
                    per_part = n_groups // zero_parts
                    pool.wait_ge(s_hn, part * per_part + 1 + n * per_part // len(beside))
                    pool.sem_inc(s_go, 1)
                    pool.dma_start(tables[k][:, :].rearrange("(p n) f -> p n f", p=NODE_P)[:, bass.ds(part * zero_n, zero_n), :],
                                   zeros.rearrange("p (n f) -> p n f", f=F)).then_inc(s_zero[k], 16)
            for b in range(DEEP):
                pool.wait_ge(s_hst[b], 16 * (n_groups // DEEP))
            pool.memset(h_parts[:, :, :, :, :], 0.0).then_inc(s_pool, 1)

            def phase_b(anywhere):
                def gather(p, q):
                    wait_for(pool, s_dst[q], p.over(2), 16, 16)
                    wait_for(pool, s_ph, p, 2, -2)
                    pool.sem_inc(s_go, 1)
                    for k in range(TILES_P):
                        pool.indirect_dma_start(out=win[:, q, k, :], out_offset=None, in_=h3[:, :],
                                                in_offset=bass.IndirectOffsetOnAxis(ap=dst_p[:, q, k:k + 1], axis=0),
                                                ).then_inc(s_win[q], 16)

                def scatter(p, q, adds):
                    for v in range(UNITS_P):
                        wait_for(pool, s_idx, p, 2, v + 1)
                        wait_for(pool, s_ysb, p, 2, v + 1)
                        for k in range(v * TILES_U, (v + 1) * TILES_U):
                            table, before = adds(k)
                            wait_for(pool, s_scat[table], before, 16)
                            pool.sem_inc(s_rot if k % TILES_U == TILES_U - 1 else s_go, 1)
                            pool.indirect_dma_start(out=tables[table][:, :],
                                                    out_offset=bass.IndirectOffsetOnAxis(ap=row_idx[:, q, k:k + 1], axis=0),
                                                    in_=y_sb[:, q, k, :], in_offset=None,
                                                    compute_op=ALU.add).then_inc(s_scat[table], 16)

                def first_pair(i, c, more=True):
                    p = Count(c, 2, i)
                    if anywhere and more:
                        gather(Count(c + 1, 2, i), (c + 1) % 2)
                    scatter(p, c % 2, lambda k: (k % FIRST_TABLES, Count(2 * c + k // FIRST_TABLES, 4, i)))

                def later_pairs(i, count=pass_pairs, base=few_pairs):
                    for c in range(count):
                        def adds(k):
                            tile = (base - few_pairs + c) * TILES_P + k
                            table = tile % TABLES
                            return table, Count(first_adds[table] + tile // TABLES, pass_pairs * TILES_P // TABLES, i)
                        q = (base + c) % 2
                        if anywhere and base + c + 1 < n_pairs:
                            gather(Count(base + c + 1, pass_pairs, i), 1 - q)
                        scatter(Count(base + c, pass_pairs, i), q, adds)

                for k in range(FIRST_TABLES):
                    pool.wait_ge(s_zero[k], 16 if k < AHEAD_TABLES else 16 * zero_parts)
                if anywhere:
                    gather(Count(0), 0)
                    gather(Count(1), 1)
                first_pair(None, 0, more=False)
                with pool.Fori(1, few_pairs // 2 + 1) as i:
                    first_pair(i, -1)
                    first_pair(i, 0)
                for k in range(FIRST_TABLES, TABLES):
                    pool.wait_ge(s_zero[k], 16 * zero_parts)
                later_pairs(None)
                with pool.Fori(1, (n_pairs - 1 - few_pairs) // pass_pairs) as i:
                    later_pairs(i)
                if scattered == n_pairs:
                    later_pairs(None, 1, n_pairs - 1)

            either(pool, phase_b)
            pool.wait_ge(s_ysb, n_units)
            for k in range(TABLES):
                pool.wait_ge(s_scat[k], 16 * adds_to[k])

            def node_loads(st):
                wait_for(pool, s_aT, st.at(), 1, 1 - DEEP)
                pool.sem_inc(s_go, 1)
                for k in range(TABLES // 2, TABLES):
                    pool.dma_start(tab_in[:, st.deep(), k, :, :],
                                   tab_view[k][:, bass.ds(st.at().value() * NODE_G, NODE_G), :]).then_inc(s_tab2[st.deep()], 16)

            loop(pool, node_loads, n_groups, 0)

        @block.scalar
        def _(act):
            act.dma_start(seg_i[:, 1, :], t["dst_seg"]).then_inc(s_seg[1], 16)
            act.wait_ge(s_x, 16 * 3)
            act.dma_start(seg_i[:, 0, :], t["src_seg"]).then_inc(s_seg[0], 16)
            act.dma_start(meta[:, SRC, :].bitcast(I32), t["src_col"]).then_inc(s_meta, 16)
            act.dma_start(meta[:, WEIGHT, :], t["weight_col"]).then_inc(s_meta, 16)
            act.wait_ge(s_mv, rows_l // STATS_G)
            act.activation(rstd[:, :], mean_var[:, :, 1], ACT.Sqrt, bias=eps[0:NODE_P, :]).then_inc(s_sqrt, 1)
            act.wait_ge(s_shift, 1)

            def normalize(g, b):
                wait_for(act, s_hT, g, 1, -1)
                for k in range(NODE_G):
                    n = bass.ds(g.value(NODE_G, k), 1)
                    last = act.activation(hn[:, b, k, :], x_all[:, n, :].rearrange("p a f -> p (a f)"),
                                          ACT.Relu, bias=shift[:, n], scale=rstd[:, n])
                last.then_inc(s_hn, 1)

            def first_part(g, b, deep):
                wait_for(act, s_hm, g, 1, 1)
                wait_for(act, s_hst[deep], g.over(DEEP), 16)
                act.copy(h_parts[:, deep, :, 0, :], p_w[b][0:NODE_P, :, :]).then_inc(s_h0, 1)

            def second_part(g, b, deep):
                wait_for(act, s_hr, g, 1, 1)
                act.copy(h_parts[:, deep, :, 1, :], h_rest[:, b, :, :]).then_inc(s_h1, 1)

            def phase_a(st):
                if st.has(0):
                    normalize(st.at(), st.v())
                if st.has(3):
                    first_part(st.at(3), st.v(3), st.deep(3))
                if st.has(4):
                    second_part(st.at(4), st.v(4), st.deep(4))

            loop(act, phase_a, n_groups, 4)

            def gelu_of(n, v):
                wait_for(act, s_z, n, 1, 1)
                wait_for(act, s_smu, n, 1, -1)
                act.activation(gelu[:, v, :], p_z[:, :], ACT.Gelu, scale=SMU_S).then_inc(s_gelu, 1)

            def weigh(n, p, q, v):
                wait_for(act, s_ph, n, 1, 1)
                wait_for(act, s_metap, p, 1, 1)
                wait_for(act, s_msg, n, 1, -1)
                for k in range(TILES_U):
                    kk = v * TILES_U + k
                    last = act.activation(hg[:, v, k, :], p_h[:, k, :], ACT.Copy, scale=meta_p[:, q, WEIGHT, kk:kk + 1])
                last.then_inc(s_hg, 1)

            def rows_out(n, q, v):
                wait_for(act, s_idx, n, 1, 1)
                wait_for(act, s_rot, n, 1, -1)
                act.copy(y_sb[:, q, v * TILES_U:(v + 1) * TILES_U, :], p_y[v][:, :, 0:F]).then_inc(s_ysb, 1)

            def step(st):
                if st.has(0):
                    gelu_of(st.at(), st.v())
                if st.has(1):
                    weigh(st.at(1), st.pair(1), st.q(1), st.v(1))
                if st.has(2):
                    rows_out(st.at(2), st.q(2), st.v(2))

            loop(act, step, n_units, 2)

            def gelu_out(g, b):
                wait_for(act, s_u, g, 1, 1)
                wait_for(act, s_os, g, 1, -1)
                act.activation(attr[:, 0, b * BANK:b * BANK + GROUP], p_y[b][:, 2:4, :].rearrange("p a n -> p (a n)")[:, 0:GROUP],
                               ACT.Gelu, scale=SMU_S).then_inc(s_oe, 1)

            def sums_out(g, b):
                wait_for(act, s_aT, g, 1, 1)
                wait_for(act, s_u, g, 1, -1)
                act.copy(hT[:, b, :, :], p_w[b][:, :, 0:NODE_P]).then_inc(s_aTs, 1)

            def node_stores(g):
                wait_for(act, s_of, g, 1, 2)
                act.sem_inc(s_carry_a, 1)
                rows = bass.ds(g.value(NODE_G), 2 * NODE_G)
                for lo, hi in lots:
                    act.dma_start(out_rows[lo:hi, rows, :], x_all[lo:hi, rows, :]).then_inc(s_out, 16)

            def phase_c(st):
                if st.has(2):
                    gelu_out(st.at(2), st.v(2))
                if st.has(1):
                    sums_out(st.at(1), st.v(1))
                if st.has(4) and st.v() == 1:
                    node_stores(st.at(5))

            loop(act, phase_c, n_groups, 4)
            act.dma_start(t["out"][full_lanes * rows_l:n_nodes, :].rearrange("(p n) f -> p n f", p=1),
                          x_all[full_lanes:full_lanes + 1, 0:last_rows, :]).then_inc(s_out, 16)

        @block.vector
        def _(dve):
            n_red = [0]

            def link(ins):
                ins.then_inc(s_red, 1)
                n_red[0] += 1
                dve.wait_ge(s_red, n_red[0])

            dve.memset(x_all[full_lanes // 32 * 32:, last_rows:, :], 0.0).then_inc(s_zeros, 1)
            dve.memset(win[:, :, :, :], 0.0).then_inc(s_zeros, 1)
            dve.memset(eps[:, :], EPS)
            dve.wait_ge(s_seg[1], 16)
            pairs_of = seg_i[:, 1, :].rearrange("p (a e) -> p a e", e=PAIR)
            dve.tensor_reduce(seg_min[:, 0, :], pairs_of, axis=AX.X, op=ALU.min)
            link(dve.tensor_reduce(seg_min[:, 1, :], pairs_of, axis=AX.X, op=ALU.max))
            link(dve.tensor_scalar(seg_min[:, 0, :], seg_min[:, 0, :], float(n_pad - WINDOW), None, ALU.min))
            link(dve.tensor_tensor(seg_min[:, 1, :], seg_min[:, 1, :], seg_min[:, 0, :], ALU.subtract))
            dve.tensor_copy(seg_win[:, :, :], seg_min[:, :, :]).then_inc(s_seg_win, 1)
            dve.wait_ge(s_x, 16 * 3)

            def node_stats(st):
                if st.has(2):
                    wait_for(dve, s_ag, st.at(2), 1, 1)
                    dve.tensor_copy(mean_var[:, bass.ds(st.at(2).value(STATS_G), STATS_G), :],
                                    mean_var_g[:, st.v(2), :, :]).then_inc(s_mv, 1)
                if st.has(0):
                    for k in range(STATS_G):
                        last = dve.bn_stats(stats[:, st.v(), k, :],
                                            x_all[:, bass.ds(st.at().value(STATS_G, k), 1), :].rearrange("p a f -> p (a f)"))
                    last.then_inc(s_st, 1)
                if st.has(1):
                    wait_for(dve, s_st, st.at(1), 1, 1)
                    wait_for(dve, s_mv, st.at(1), 1, -1)
                    dve.sem_inc(s_carry_v, 1)
                    for k in range(STATS_G):
                        last = dve.bn_aggr(mean_var_g[:, st.v(1), k, :], stats[:, st.v(1), k, :])
                    last.then_inc(s_ag, 1)

            loop(dve, node_stats, rows_l // STATS_G, 2, body=2)
            dve.wait_ge(s_meta, 32)
            dve.tensor_copy(meta[:, SRC, :], meta[:, SRC, :].bitcast(I32))
            dve.wait_ge(s_sqrt, 1)
            link(dve.reciprocal(rstd[:, :], rstd[:, :]))
            dve.scalar_tensor_tensor(shift[:, :], mean_var[:, :, 0], -1.0, rstd[:, :], ALU.mult, ALU.mult).then_inc(s_shift, 1)
            dve.wait_ge(s_ld, 16 * N_LD)
            for part in range(PARTS - 1):
                link(dve.tensor_copy(bias_part[0:1, part, :, :], bias[0:1, part, :, :]))
                link(dve.tensor_tensor(bias[0:1, part + 1, :, :], bias[0:1, part, :, :], bias_part[0:1, part, :, :], ALU.subtract))
            dve.tensor_copy(bias_part[0:1, PARTS - 1, :, :], bias[0:1, PARTS - 1, :, :]).then_inc(s_parts, 1)
            dve.tensor_scalar(w_f2[:, :], w_f2[:, :], SMU_W, None, ALU.mult)
            dve.tensor_scalar(w_o2[:, :], w_o2[:, :], SMU_W, None, ALU.mult)
            dve.wait_ge(s_pool, 5)
            link(dve.tensor_scalar(tie_limit[:, :].bitcast(I32), lane[:, :], -1.0, 190.0, ALU.mult, ALU.add))
            link(dve.tensor_scalar(tie_weight[:, :].bitcast(I32), tie_limit[:, :].bitcast(I32), 23, None,
                                   ALU.logical_shift_left))
            dve.tensor_scalar(tie_limit[:, :], tie_weight[:, :], 2.5, None, ALU.mult)
            dve.tensor_scalar(dump_row[:, :], lane[:, :], float(dump), None, ALU.add)
            dve.tensor_copy(msg[:, :, :, F].rearrange("p a b -> p (a b)"),
                            tie_weight[:, :].to_broadcast([LANES, 2 * TILES_U])).then_inc(s_scaled, 1)
            dve.wait_ge(s_win_ld, 32)
            dve.tensor_scalar(win_row[:, :], win_i[:, :], lane[:, :], None, ALU.add)
            link(dve.tensor_reduce(reach[:, :], win_first[:, 1, :], axis=AX.X, op=ALU.max))
            dve.tensor_scalar(general[:, :], reach[:, :], float(WINDOW) - 0.5, None, ALU.is_gt).then_inc(s_flag, 1)

            def transposed(g, b):
                wait_for(dve, s_hT, g, 1, 1)
                wait_for(dve, s_hm, g, 1, -1)
                dve.tensor_copy(hT[:, b, :, :], p_y[b][:, 0:2, :].rearrange("p a (two n) -> p (a two) n", two=2)[:, :, 0:NODE_P]).then_inc(s_hTs, 1)

            def rest_of_h(g, b, deep):
                wait_for(dve, s_h2, g, 1, -1)
                wait_for(dve, s_h0, g, 1, 1)
                dve.tensor_tensor(h_rest[:, b, :, :], p_w[b][0:NODE_P, :, :], h_parts[:, deep, :, 0, :], ALU.subtract).then_inc(s_hr, 1)

            def third_part(g, b, deep):
                wait_for(dve, s_h1, g, 1, 1)
                dve.tensor_tensor(h_parts[:, deep, :, 2, :], h_rest[:, b, :, :], h_parts[:, deep, :, 1, :], ALU.subtract).then_inc(s_h2, 1)

            def phase_a(st):
                if st.has(4):
                    rest_of_h(st.at(4), st.v(4), st.deep(4))
                if st.has(1):
                    transposed(st.at(1), st.v(1))
                if st.has(5):
                    third_part(st.at(5), st.v(5), st.deep(5))

            loop(dve, phase_a, n_groups, 5)
            dve.wait_ge(s_flag, 1)
            dve.wait_ge(s_e16, 32)

            def phase_b(anywhere):
                def pair_meta(p, q):
                    wait_for(dve, s_idx, p, 2, -2)
                    tiles = bass.ds(p.value() * TILES_P, TILES_P)
                    dve.tensor_copy(meta_p[:, q, 0:2, :], meta[:, :, tiles])
                    dve.tensor_scalar(meta_p[:, q, DUMP, :], meta[:, SRC, tiles], -1.0, dump_row[:, :], ALU.mult, ALU.add
                                      ).then_inc(s_metap, 1)

                def smu(n, v):
                    wait_for(dve, s_gelu, n, 1, 1)
                    wait_for(dve, s_w, n, 1, -1)
                    dve.scalar_tensor_tensor(act1[:, v, :], p_z[:, :], SMU_L, gelu[:, v, :], ALU.mult, ALU.add).then_inc(s_smu, 1)

                def message(n, v):
                    wait_for(dve, s_hg, n, 1, 1)
                    wait_for(dve, s_w, n, 1, 1)
                    wait_for(dve, s_y, n, 1, -1)
                    dve.tensor_tensor(msg[:, v, :, 0:F], p_w[v][:, :, :], hg[:, v, :, :], ALU.mult).then_inc(s_msg, 1)

                def row_numbers(n, q, v):
                    cols = slice(v * TILES_U, (v + 1) * TILES_U)
                    wait_for(dve, s_y, n, 1, 1)
                    wait_for(dve, s_rot, n, 1, -1)
                    dve.scalar_tensor_tensor(redirect[:, v, :], p_y[v][:, :, F], tie_limit[:, :], meta_p[:, q, DUMP, cols],
                                             ALU.is_gt, ALU.mult).then_inc(s_tie, 1)
                    wait_for(dve, s_tie, n, 1, 1)
                    dve.tensor_tensor(row_idx[:, q, cols], redirect[:, v, :], meta_p[:, q, SRC, cols], ALU.add).then_inc(s_idx, 1)

                def pick_target(n, p, q, v):
                    wait_for(dve, s_ph, n, 1, -1)
                    dve.tensor_scalar(pick[:, v, :], ends[:, q, 1, v * UNIT:(v + 1) * UNIT], win_row[:, bass.ds(p.value(), 1)], None,
                                      ALU.is_equal).then_inc(s_pick, 1)

                def same_source(n, q, v):
                    wait_for(dve, s_y, n, 1, -1)
                    dve.tensor_tensor(same[:, v, :, :],
                                      ends[:, q, 0, v * UNIT:(v + 1) * UNIT].rearrange("p (k e) -> p k e", k=TILES_U),
                                      meta_p[:, q, SRC, v * TILES_U:(v + 1) * TILES_U].unsqueeze(2).to_broadcast([LANES, TILES_U, LANES]),
                                      ALU.is_equal).then_inc(s_same, 1)

                def step(st):
                    if st.has(0) and st.v() == 0:
                        pair_meta(st.pair(), st.q())
                        wait_for(dve, s_ends[st.q()], st.pair().over(2), 16, 16)
                        wait_for(dve, s_metap, st.pair(), 1, 1)
                    if st.has(0):
                        smu(st.at(), st.v())
                        if not anywhere:
                            pick_target(st.at(), st.pair(), st.q(), st.v())
                    if st.has(1):
                        message(st.at(1), st.v(1))
                    if st.has(2):
                        row_numbers(st.at(2), st.q(2), st.v(2))
                    if st.has(0):
                        same_source(st.at(), st.q(), st.v())

                loop(dve, step, n_units, 2)

            either(dve, phase_b)

            def sum_tables(g, deep):
                for loads, n_loads in ((s_tab, TABLES // 2), (s_tab2, TABLES - TABLES // 2)):
                    wait_for(dve, loads[deep], g.over(DEEP), 16 * n_loads, 16 * n_loads)
                for k in range(1, DVE_TABLES):
                    if k > 1:
                        wait_for(dve, s_sum, g, DVE_TABLES - 1, k - 1)
                    dve.tensor_tensor(tab_in[:, deep, 0, :, :], tab_in[:, deep, 0, :, :], tab_in[:, deep, k, :, :],
                                      ALU.add).then_inc(s_sum, 1)

            def smu_out(g, b):
                wait_for(dve, s_oe, g, 1, 1)
                wait_for(dve, s_om, g, 1, -1)
                dve.scalar_tensor_tensor(attr[:, 1, b * BANK:b * BANK + GROUP],
                                         p_y[b][:, 2:4, :].rearrange("p a n -> p (a n)")[:, 0:GROUP], SMU_L,
                                         attr[:, 0, b * BANK:b * BANK + GROUP], ALU.mult, ALU.add).then_inc(s_os, 1)

            def output(g, b):
                wait_for(dve, s_om, g, 1, 1)
                rows = bass.ds(g.value() * NODE_G, NODE_G)
                dve.tensor_tensor(x_all[:, rows, :], p_y[b][0:NODE_P, 0:2, :].rearrange("p a (two n) -> p (a two) n", two=2),
                                  x_all[:, rows, :], ALU.add).then_inc(s_of, 1)

            def phase_c(st):
                if st.has(0):
                    sum_tables(st.at(), st.deep())
                if st.has(2):
                    smu_out(st.at(2), st.v(2))
                if st.has(3):
                    output(st.at(3), st.v(3))

            loop(dve, phase_c, n_groups, 3)

        @block.tensor
        def _(pe):
            pe.wait_ge(s_ld, 16 * N_LD)
            pe.wait_ge(s_pool, 5)

            def transpose_nodes(g, b):
                wait_for(pe, s_hn, g, 1, 1)
                wait_for(pe, s_hTs, g, 1, -1)
                for k in range(NODE_G):
                    last = pe.transpose(p_y[b][:, k // 2, k % 2 * LANES:k % 2 * LANES + NODE_P], hn[:, b, k, :],
                                        ident[0:NODE_P, 0:NODE_P])
                last.then_inc(s_hT, 1)

            def first_layer(g, b):
                wait_for(pe, s_hTs, g, 1, 1)
                wait_for(pe, s_hr, g, 1, -1)
                for k in range(NODE_G):
                    last = pe.matmul(p_w[b][0:NODE_P, k, :], hT[:, b, k, :], w_in[:, :], start=True, stop=True)
                last.then_inc(s_hm, 1)

            def phase_a(st):
                if st.has(1):
                    transpose_nodes(st.at(1), st.v(1))
                if st.has(2):
                    first_layer(st.at(2), st.v(2))

            loop(pe, phase_a, n_groups, 2)
            pe.wait_ge(s_h2, n_groups)
            pe.wait_ge(s_scaled, 1)
            pe.wait_ge(s_moved, 16 * PARTS * BIASES)

            def phase_b(anywhere):
                def filter2(n, v):
                    wait_for(pe, s_smu, n, 1, 1)
                    wait_for(pe, s_msg, n, 1, -1)
                    pe.matmul(p_w[v][:, :, :], ones_bf[:, 0:LANES], bias_rows[:, B_F2, :, :], start=True, stop=False)
                    for k in range(TILES_U):
                        last = pe.matmul(p_w[v][:, k, :], act1[:, v, k * LANES:(k + 1) * LANES], w_f2[:, :],
                                         start=False, stop=(k == TILES_U - 1))
                    last.then_inc(s_w, 1)

                def filter1(n, p, q, v):
                    if v == 0:
                        wait_for(pe, s_attr[q], p.over(2), 16, 16)
                    wait_for(pe, s_smu, n)
                    pe.matmul(p_z[:, :], w_f1[:, :], attr[:, q, v * UNIT:(v + 1) * UNIT], start=True, stop=True).then_inc(s_z, 1)

                def targets(n, p, q, v):
                    if v == 0:
                        count = 16 * TILES_P if anywhere else 16
                        wait_for(pe, s_win[q], p.over(2), count, count)
                    if not anywhere:
                        wait_for(pe, s_pick, n, 1, 1)
                    wait_for(pe, s_hg, n)
                    for k in range(TILES_U):
                        which = ident_bf[:, :] if anywhere else pick[:, v, k * LANES:(k + 1) * LANES]
                        for part in range(PARTS):
                            rows = win[:, q, v * TILES_U + k if anywhere else window_slot[q], part * F:(part + 1) * F]
                            last = pe.matmul(p_h[:, k, :], which, rows, start=(part == 0), stop=(part == PARTS - 1))
                    last.then_inc(s_ph, 1)

                def sum_same(n, v):
                    wait_for(pe, s_msg, n, 1, 1)
                    wait_for(pe, s_same, n, 1, 1)
                    wait_for(pe, s_ysb, n, 1, -1)
                    for k in range(TILES_U):
                        last = pe.matmul(p_y[v][:, k, 0:FT], same[:, v, k, :], msg[:, v, k, :], start=True, stop=True)
                    last.then_inc(s_y, 1)

                def step(st):
                    if st.has(1):
                        filter2(st.at(1), st.v(1))
                    if st.has(0):
                        filter1(st.at(), st.pair(), st.q(), st.v())
                    if st.has(1):
                        targets(st.at(1), st.pair(1), st.q(1), st.v(1))
                    if st.has(2):
                        sum_same(st.at(2), st.v(2))

                loop(pe, step, n_units, 2)

            either(pe, phase_b)

            pe.wait_ge(s_ysb, n_units)

            def transpose_sums(g, b, deep):
                for loads, n_loads in ((s_tab, TABLES // 2), (s_tab2, TABLES - TABLES // 2)):
                    wait_for(pe, loads[deep], g.over(DEEP), 16 * n_loads, 16 * n_loads)
                wait_for(pe, s_sum, g, DVE_TABLES - 1, DVE_TABLES - 1)
                wait_for(pe, s_aTs, g, 1, -1)
                left = [0] + list(range(DVE_TABLES, TABLES))
                for k in range(NODE_G):
                    for n, j in enumerate(left):
                        last = pe.matmul(p_w[b][:, k, 0:NODE_P], tab_in[:, deep, j, k, :], ident[0:NODE_P, 0:NODE_P],
                                         start=(n == 0), stop=(n == len(left) - 1))
                last.then_inc(s_aT, 1)

            def hidden(g, b):
                wait_for(pe, s_aTs, g, 1, 1)
                wait_for(pe, s_os, g, 1, -1)
                out = p_y[b][:, 2:4, :].rearrange("p a n -> p (a n)")[:, 0:GROUP]
                pe.matmul(out, bias_rows[:, B_O1, 0, :], ones_bf[:, 0:GROUP], start=True, stop=False)
                pe.matmul(out, w_o1[:, :], hT[:, b, :, :], start=False, stop=True).then_inc(s_u, 1)

            def last_layer(g, b):
                wait_for(pe, s_os, g, 1, 1)
                wait_for(pe, s_of, g, 1, -1)
                pe.matmul(p_y[b][0:NODE_P, 0:2, :].rearrange("p a n -> p (a n)"), ones_bf[:, 0:NODE_P],
                          bias_rows[:, B_O2, :, :].rearrange("p k f -> p (k f)"), start=True, stop=False)
                for k in range(NODE_G):
                    last = pe.matmul(p_y[b][0:NODE_P, k // 2, k % 2 * LANES:k % 2 * LANES + F],
                                     attr[:, 1, b * BANK + k * NODE_P:b * BANK + (k + 1) * NODE_P], w_o2[:, :],
                                     start=False, stop=(k == NODE_G - 1))
                last.then_inc(s_om, 1)

            def phase_c(st):
                if st.has(3):
                    last_layer(st.at(3), st.v(3))
                if st.has(2):
                    hidden(st.at(2), st.v(2))
                if st.has(1):
                    transpose_sums(st.at(1), st.v(1), st.deep(1))

            loop(pe, phase_c, n_groups, 3)


def kernel(**inputs):
    import concourse.bacc as bacc
    from concourse.bass_utils import run_bass_kernel_spmd as run

    x = np.asarray(inputs["x"])
    n_nodes, F = x.shape
    attr = np.asarray(inputs["edge_attr_20"])
    n_edges, R = attr.shape
    padded = -(-n_edges // (BODY * UNIT)) * (BODY * UNIT)

    def pad(a):
        out = np.zeros((padded,) + a.shape[1:], a.dtype)
        out[:n_edges] = a
        return out

    def col(a):
        return np.ascontiguousarray(a.reshape(-1, LANES).T)

    src, dst = pad(np.asarray(inputs["src"])), pad(np.asarray(inputs["dst"]))
    dst[n_edges:] = dst[n_edges - 1]
    g = {k[len("L0_gnn_"):]: np.asarray(v) for k, v in inputs.items() if k.startswith("L0_gnn_")}
    arrays = {
        "x": np.ascontiguousarray(x),
        "attrT": np.ascontiguousarray(pad(attr).T),
        "src_seg": src.reshape(-1, 4 * PAIR),
        "dst_seg": dst.reshape(-1, 4 * PAIR),
        "src_col": col(src),
        "dst_col": col(dst),
        "weight_col": col(pad(np.asarray(inputs["edge_weight"]))),
        "w_inT": np.ascontiguousarray(g["W_in2f"].T),
        "w_f1T": np.ascontiguousarray(g["W_f1"].T),
        "w_f2T": np.ascontiguousarray(g["W_f2"].T),
        "w_o1T": np.ascontiguousarray(g["W_o1"].T),
        "w_o2T": np.ascontiguousarray(g["W_o2"].T),
        "b_f1": g["b_f1"].reshape(1, F),
        "biases": np.concatenate([g["b_f2"], g["b_o1"], g["b_o2"]]).reshape(1, 3, F),
    }
    nc = bacc.Bacc("TRN2", target_bir_lowering=False, num_devices=1)
    t = {k: nc.dram_tensor(f"in_{k}", a.shape, mybir.dt.from_np(a.dtype), kind="ExternalInput").ap()
         for k, a in arrays.items()}
    t["out"] = nc.dram_tensor("out", (n_nodes, F), F32, kind="ExternalOutput").ap()
    build(nc, n_nodes, padded, n_edges, F, R, t)
    r = run(nc, [{f"in_{k}": a for k, a in arrays.items()}], core_ids=[0])
    return r.results[0]["out"]
```
